# Optimizing a Trainium2 kernel written in Bass

```python
import numpy as np
import jax
import jax.numpy as jnp

def _softmax(x, axis=-1):
    return jax.nn.softmax(x, axis=axis)

def _gelu(x):
    return jax.nn.gelu(x, approximate=True)

def _silu(x):
    return jax.nn.silu(x)

def _sigmoid(x):
    return jax.nn.sigmoid(x)

def _layernorm(x, axis=-1, eps=1e-05):
    m = jnp.mean(x, axis=axis, keepdims=True)
    v = jnp.var(x, axis=axis, keepdims=True)
    return (x - m) / jnp.sqrt(v + eps)

def _scatter_add(tgt, idx, src, axis=0):
    return tgt.at[idx].add(src)

def _segment_sum(src, seg, n):
    return jax.ops.segment_sum(src, seg, n)
kernel_name = 'mk_seq_preln_d1_jaxref_r8_c68e51'

def setup_inputs(seed: int=0):
    np.random.seed(seed)
    _w = jnp.asarray

    def _L0_attn_setup():
        import jax, jax.numpy as jnp
        import numpy as np
        HIDDEN = 512
        HEAD_DIM = 128
        N_Q_HEADS = 32
        N_KV_HEADS = 8
        SLIDING_WINDOW = 128
        ROPE_THETA = 10000.0
        BATCH, SEQ = (1, 256)

        def _rope(t, pos):
            d = t.shape[-1]
            half = d // 2
            inv_freq = ROPE_THETA ** (-jnp.arange(half, dtype=jnp.float32) / half)
            ang = pos[:, None].astype(jnp.float32) * inv_freq[None, :]
            cos = jnp.cos(ang)[None, :, None, :]
            sin = jnp.sin(ang)[None, :, None, :]
            t1, t2 = (t[..., :half], t[..., half:])
            return jnp.concatenate([t1 * cos - t2 * sin, t1 * sin + t2 * cos], axis=-1)
        key = jax.random.key(seed)
        ks = jax.random.split(key, 5)
        w_scale = HIDDEN ** (-0.5)
        return {'x': jax.random.normal(ks[0], (BATCH, SEQ, HIDDEN), jnp.float32), 'wq': jax.random.normal(ks[1], (HIDDEN, N_Q_HEADS * HEAD_DIM), jnp.float32) * w_scale, 'wk': jax.random.normal(ks[2], (HIDDEN, N_KV_HEADS * HEAD_DIM), jnp.float32) * w_scale, 'wv': jax.random.normal(ks[3], (HIDDEN, N_KV_HEADS * HEAD_DIM), jnp.float32) * w_scale, 'wo': jax.random.normal(ks[4], (N_Q_HEADS * HEAD_DIM, HIDDEN), jnp.float32) * w_scale}
    _L0_attn_in = _L0_attn_setup()

    def _L0_ffn_setup():
        import jax, jax.numpy as jnp
        import numpy as np
        B, S, D, O, E, R = (4, 256, 512, 512, 8, 16)
        SCALING = 32.0 / 16.0
        MAX_THRESHOLD = 0.125
        key = jax.random.key(seed)
        ks = jax.random.split(key, 8)
        return {'x': jax.random.normal(ks[0], (B, S, D), jnp.float32), 'W_base': jax.random.normal(ks[1], (O, D), jnp.float32) * (1.0 / np.sqrt(D)), 'b_base': jax.random.normal(ks[2], (O,), jnp.float32) * 0.02, 'W_gate': jax.random.normal(ks[3], (E, D), jnp.float32) * (1.0 / np.sqrt(D)), 'W_thr': jax.random.normal(ks[4], (D,), jnp.float32) * (1.0 / np.sqrt(D)), 'b_thr': jax.random.normal(ks[5], (1,), jnp.float32) * 0.02, 'A_w': jax.random.normal(ks[6], (E, R, D), jnp.float32) * (1.0 / np.sqrt(D)), 'B_w': jax.random.normal(ks[7], (E, O, R), jnp.float32) * (1.0 / np.sqrt(R))}
    _L0_ffn_in = _L0_ffn_setup()
    _d = {'L0_attn_x': _L0_attn_in['x'], 'L0_attn_wq': _L0_attn_in['wq'], 'L0_attn_wk': _L0_attn_in['wk'], 'L0_attn_wv': _L0_attn_in['wv'], 'L0_attn_wo': _L0_attn_in['wo'], 'L0_ffn_W_base': _L0_ffn_in['W_base'], 'L0_ffn_b_base': _L0_ffn_in['b_base'], 'L0_ffn_W_gate': _L0_ffn_in['W_gate'], 'L0_ffn_W_thr': _L0_ffn_in['W_thr'], 'L0_ffn_b_thr': _L0_ffn_in['b_thr'], 'L0_ffn_A_w': _L0_ffn_in['A_w'], 'L0_ffn_B_w': _L0_ffn_in['B_w']}
    _x0 = _d['L0_attn_x']
    _d['L0_attn_x'] = jax.random.normal(jax.random.fold_in(jax.random.key(seed), 1), (2, 512, 512), dtype=_x0.dtype)
    del _x0
    return _d

def reference(L0_attn_x, L0_attn_wq, L0_attn_wk, L0_attn_wv, L0_attn_wo, L0_ffn_W_base, L0_ffn_b_base, L0_ffn_W_gate, L0_ffn_W_thr, L0_ffn_b_thr, L0_ffn_A_w, L0_ffn_B_w):

    def _L0_attn_ref(x, wq, wk, wv, wo):
        import jax, jax.numpy as jnp
        import numpy as np
        HIDDEN = 512
        HEAD_DIM = 128
        N_Q_HEADS = 32
        N_KV_HEADS = 8
        SLIDING_WINDOW = 128
        ROPE_THETA = 10000.0
        BATCH, SEQ = (1, 256)

        def _rope(t, pos):
            d = t.shape[-1]
            half = d // 2
            inv_freq = ROPE_THETA ** (-jnp.arange(half, dtype=jnp.float32) / half)
            ang = pos[:, None].astype(jnp.float32) * inv_freq[None, :]
            cos = jnp.cos(ang)[None, :, None, :]
            sin = jnp.sin(ang)[None, :, None, :]
            t1, t2 = (t[..., :half], t[..., half:])
            return jnp.concatenate([t1 * cos - t2 * sin, t1 * sin + t2 * cos], axis=-1)
        B, S, _ = x.shape
        G = N_Q_HEADS // N_KV_HEADS
        sm_scale = HEAD_DIM ** (-0.5)
        q = (x @ wq).reshape(B, S, N_Q_HEADS, HEAD_DIM)
        k = (x @ wk).reshape(B, S, N_KV_HEADS, HEAD_DIM)
        v = (x @ wv).reshape(B, S, N_KV_HEADS, HEAD_DIM)
        pos = jnp.arange(S)
        q = _rope(q, pos)
        k = _rope(k, pos)
        qg = q.reshape(B, S, N_KV_HEADS, G, HEAD_DIM)
        scores = jnp.einsum('bqhgd,bshd->bhgqs', qg, k) * sm_scale
        i = pos[:, None]
        j = pos[None, :]
        allowed = (j <= i) & (j > i - SLIDING_WINDOW)
        neg = jnp.finfo(scores.dtype).min
        scores = jnp.where(allowed[None, None, None], scores, neg)
        attn = jax.nn.softmax(scores, axis=-1)
        out = jnp.einsum('bhgqs,bshd->bqhgd', attn, v).reshape(B, S, N_Q_HEADS * HEAD_DIM)
        return out @ wo

    def _L0_ffn_ref(x, W_base, b_base, W_gate, W_thr, b_thr, A_w, B_w):
        import jax, jax.numpy as jnp
        import numpy as np
        B, S, D, O, E, R = (4, 256, 512, 512, 8, 16)
        SCALING = 32.0 / 16.0
        MAX_THRESHOLD = 0.125
        base = jnp.einsum('bsd,od->bso', x, W_base) + b_base
        xf = x.reshape(-1, D)
        gate = jax.nn.softmax(xf @ W_gate.T, axis=-1)
        thr = jax.nn.sigmoid(xf @ W_thr + b_thr[0]) * MAX_THRESHOLD
        adapted = gate - thr[:, None]
        selected = (adapted >= 0).astype(x.dtype)
        w = adapted * selected
        wsum = jnp.sum(w, axis=-1, keepdims=True)
        wsum = jnp.where(wsum == 0, jnp.ones_like(wsum), wsum)
        w = w / wsum
        h = jnp.einsum('nd,erd->ner', xf, A_w)
        moe = jnp.einsum('ner,ne,eor->no', h, w, B_w) * SCALING
        return base + moe.reshape(base.shape)
    x = L0_attn_x
    x = x + _L0_attn_ref(_layernorm(x, axis=-1), L0_attn_wq, L0_attn_wk, L0_attn_wv, L0_attn_wo)
    x = x + _L0_ffn_ref(_layernorm(x, axis=-1), L0_ffn_W_base, L0_ffn_b_base, L0_ffn_W_gate, L0_ffn_W_thr, L0_ffn_b_thr, L0_ffn_A_w, L0_ffn_B_w)
    return x

_drawn_inputs = setup_inputs


def setup_inputs(seed=0):
    import zlib

    import numpy as np

    out = dict(_drawn_inputs(seed))
    spreads = {}
    factors = {'L0_ffn_b_base': 5.8}
    for name, (base, spread) in spreads.items():
        noise = np.random.default_rng([zlib.crc32(name.encode()), seed]).standard_normal(out[name].shape)
        drawn = base * np.exp(spread * noise) if base else spread * noise
        out[name] = jnp.asarray(drawn.astype(out[name].dtype))
    for name, factor in factors.items():
        out[name] = (out[name] * factor).astype(out[name].dtype)
    return out
```

```python
import numpy as np
import concourse.bass as bass
from concourse import mybir
from contextlib import ExitStack

F32 = mybir.dt.float32
F32R = mybir.dt.float32r
ALU = mybir.AluOpType
ACT = mybir.ActivationFunctionType
AX = mybir.AxisListType

BATCH, SEQ, HIDDEN = 2, 512, 512
HEADS, KV_HEADS, D = 32, 8, 128
PER_GROUP = HEADS // KV_HEADS
TOKENS = BATCH * SEQ
P = 128
KT = HIDDEN // P
QB = SEQ // P
BLOCKS = TOKENS // P
SM_SCALE = float(D) ** -0.5
MASKED = -1.0e38
LOWEST = -3.4e38
EPS = 1e-5
EXPERTS, RANK = 8, 16
ER = EXPERTS * RANK
GCOLS = ER + EXPERTS + 1
LORA_SCALING = 2.0
MAX_THRESHOLD = 0.125

PROJ_BEFORE = 6
PROJ_PER_GROUP = 12


def q_proj_use(g, j, t):
    return g * PROJ_PER_GROUP + (PROJ_BEFORE + (0, 2, 4, 8)[j] + t)


def k_proj_use(g, t):
    return g * PROJ_PER_GROUP + (PROJ_BEFORE + 6 + t)


def v_proj_use(g, t):
    return g * PROJ_PER_GROUP + (PROJ_BEFORE + 10 + t)


def q_rope_use(g, j, t):
    return g * 8 + (2 * j + t + 2)


def k_rope_use(g, t):
    return 2 * g + t


def trans_use(g, j, t, half):
    return g * 18 + (4 * j - 4 + (2 if j else 0) + 2 * t + half)


def v_trans_use(g, t):
    return g * 18 + t


def pv_use(g, j, t):
    if j == 1 and t == 0:
        return 0 if isinstance(g, int) and g == 0 else g * 16 - 4
    return g * 16 + ((-10, 0, 2, 4)[j] + t)


def out_use(g, b):
    behind = isinstance(g, int) and g == KV_HEADS
    return g * 16 + (b - 8 + (b >= QB and not behind))


def out_bank(g, b):
    behind = isinstance(g, int) and g == KV_HEADS
    return (b + (b >= QB and not behind)) % 2


def wait(eng, sem, count):
    if isinstance(count, int) and count <= 0:
        return
    eng.wait_ge(sem, count)


def layer_kernel(nc, x, wq, wk, wv, wo, w_base, b_base, a_gate, b_thr, b_lora, cos_t, sin_t, band, eye, out):
    ctx = ExitStack()
    with ctx:
        def sb(name, shape, dt=F32):
            return ctx.enter_context(nc.sbuf_tensor(name, shape, dt))

        def bank(name):
            return ctx.enter_context(nc.psum_tensor(name, [P, 512], F32))

        def sem(name):
            return ctx.enter_context(nc.semaphore(name))

        resid = sb("resid", [P, BLOCKS, HIDDEN])
        xT_hi = sb("xT_hi", [P, KT, TOKENS], F32R)
        xT_lo = sb("xT_lo", [P, KT, TOKENS], F32R)
        wq_raw = sb("wq_raw", [P, 2, KT * D])
        wk_raw = sb("wk_raw", [P, KT * D])
        wv_raw = sb("wv_raw", [P, KT * D])
        wo_raw = sb("wo_raw", [P, 2, HIDDEN])
        wq_hi = sb("wq_hi", [P, KT * D], F32R)
        wq_lo = sb("wq_lo", [P, KT * D], F32R)
        wk_hi = sb("wk_hi", [P, KT * D], F32R)
        wk_lo = sb("wk_lo", [P, KT * D], F32R)
        wv_hi = sb("wv_hi", [P, KT * D], F32R)
        wv_lo = sb("wv_lo", [P, KT * D], F32R)
        wo_hi = sb("wo_hi", [P, PER_GROUP, HIDDEN], F32R)
        wo_lo = sb("wo_lo", [P, PER_GROUP, HIDDEN], F32R)
        q_hi = sb("q_hi", [P, TOKENS], F32R)
        q_lo = sb("q_lo", [P, TOKENS], F32R)
        k_hi = sb("k_hi", [P, TOKENS], F32R)
        k_lo = sb("k_lo", [P, TOKENS], F32R)
        v_hi = sb("v_hi", [P, TOKENS], F32R)
        v_lo = sb("v_lo", [P, TOKENS], F32R)
        rope_cos = sb("rope_cos", [P, BATCH, SEQ])
        rope_sin = sb("rope_sin", [P, BATCH, SEQ])
        k_rot = sb("k_rot", [P, BATCH, SEQ])
        k_sin = sb("k_sin", [P, BATCH, SEQ])
        k_first = sb("k_first", [P, BATCH, P])
        vT = sb("vT", [P, BATCH, SEQ])
        probs = sb("probs", [P, 2, BLOCKS, 2 * P])
        pT_hi = sb("pT_hi", [P, BATCH, 6 * P], F32R)
        pT_lo = sb("pT_lo", [P, BATCH, 6 * P], F32R)
        oT_hi = sb("oT_hi", [P, PER_GROUP, TOKENS], F32R)
        oT_lo = sb("oT_lo", [P, PER_GROUP, TOKENS], F32R)
        v_last = sb("v_last", [P, BATCH, P])
        pT_last = sb("pT_last", [P, BATCH, P])
        cos_sb = sb("cos_sb", [P, SEQ])
        sin_sb = sb("sin_sb", [P, SEQ])
        band_sb = sb("band_sb", [P, 2 * P])
        eye_sb = sb("eye_sb", [P, P])
        row_max = sb("row_max", [P, 2, BLOCKS])
        shift = sb("shift", [P, 2, BLOCKS])
        row_sum = sb("row_sum", [P, 2, BLOCKS])
        inv_sum = sb("inv_sum", [P, 2, BLOCKS])
        stats = sb("stats", [P, BLOCKS, 6])
        moments = sb("moments", [P, BLOCKS, 2])
        rstd = sb("rstd", [P, BLOCKS])
        var_eps = sb("var_eps", [P, BLOCKS])
        gap = sb("gap", [P, 1])
        minus_half = sb("minus_half", [P, 1])
        wb_raw = probs[:, 0, :, :].rearrange("p a b -> p (a b)")
        wb_hi = (k_hi, q_hi)
        wb_lo = (k_lo, q_lo)
        normed = probs[:, 1, :, :].rearrange("p (s a) b -> p s (a b)", s=4)

        def yT(b):
            return (rope_sin if b % 4 < 2 else rope_cos)[:, b % 2, :]

        result = k_rot
        lora_h = vT[:, 0, :].rearrange("p (a b) -> p a b", a=QB)
        lora_hT = vT[:, 1, :].rearrange("p (a b) -> p a b", a=QB)
        ag_sb = sb("ag_sb", [P, KT * GCOLS])
        bl_sb = wk_raw
        bb_sb = wv_raw
        bt_sb = sb("bt_sb", [P, 1])
        logit = sb("logit", [P, QB, EXPERTS + 1])
        gmax = sb("gmax", [P, QB])
        gexp = sb("gexp", [P, QB, EXPERTS + 1])
        gate = sb("gate", [P, QB, EXPERTS])
        gsum = sb("gsum", [P, QB])
        ginv = sb("ginv", [P, QB])
        thr = sb("thr", [P, QB])
        iszero = sb("iszero", [P, QB])

        sc_bank = [bank("sc0"), bank("sc1")]
        pj_bank = [bank("pj0"), bank("pj1")]
        tr_bank = [bank("tr0"), bank("tr1")]
        o_bank = [bank("ob0"), bank("ob1")]

        x_in = [sem(f"x_in{b}") for b in range(BLOCKS)]
        eye_in = sem("eye_in")
        tables_in = sem("tables_in")
        wq_in = [sem("wq_in0"), sem("wq_in1")]
        wk_in = sem("wk_in")
        wv_in = sem("wv_in")
        wo_in = [sem("wo_in0"), sem("wo_in1")]
        wq_hi_ready = sem("wq_hi_ready")
        wq_lo_ready = sem("wq_lo_ready")
        wk_hi_ready = sem("wk_hi_ready")
        wk_lo_ready = sem("wk_lo_ready")
        wv_hi_ready = sem("wv_hi_ready")
        wv_lo_ready = sem("wv_lo_ready")
        wo_hi_ready = sem("wo_hi_ready")
        wo_lo_ready = sem("wo_lo_ready")
        ln_step = sem("ln_step")
        moments_ready = sem("moments_ready")
        var_ready = sem("var_ready")
        rstd_ready = sem("rstd_ready")
        normed_ready = sem("normed_ready")
        xT_done = sem("xT_done")
        xT_hi_ready = sem("xT_hi_ready")
        xT_lo_ready = sem("xT_lo_ready")
        proj_done = sem("proj_done")
        proj_taken = sem("proj_taken")
        rope_swapped = sem("rope_swapped")
        rope_scaled = sem("rope_scaled")
        rope_added = sem("rope_added")
        k_swapped = sem("k_swapped")
        k_scaled = sem("k_scaled")
        k_added = sem("k_added")
        q_hi_ready = sem("q_hi_ready")
        q_lo_ready = sem("q_lo_ready")
        k_hi_ready = sem("k_hi_ready")
        k_lo_ready = sem("k_lo_ready")
        v_hi_ready = sem("v_hi_ready")
        scores_done = sem("scores_done")
        scores_masked = sem("scores_masked")
        shift_ready = sem("shift_ready")
        exp_done = sem("exp_done")
        inv_ready = sem("inv_ready")
        probs0_ready = sem("probs0_ready")
        probs1_ready = sem("probs1_ready")
        trans_done = sem("trans_done")
        pT_hi_ready = sem("pT_hi_ready")
        trans_taken = sem("trans_taken")
        o_done = sem("o_done")
        oT_hi_ready = sem("oT_hi_ready")
        o_taken = sem("o_taken")
        constant_set = sem("constant_set")
        wb_in = sem("wb_in")
        lora_bias_in = sem("lora_bias_in")
        wb_hi_ready = sem("wb_hi_ready")
        wb_lo_ready = sem("wb_lo_ready")
        y_normed = sem("y_normed")
        yT_done = sem("yT_done")
        yT_ready = sem("yT_ready")
        yT_hi_ready = sem("yT_hi_ready")
        yT_lo_ready = sem("yT_lo_ready")
        bias_added = sem("bias_added")
        down_done = sem("down_done")
        logits_ready = sem("logits_ready")
        gexp_done = sem("gexp_done")
        gate_step = sem("gate_step")
        lora_scaled = sem("lora_scaled")
        loraT_done = sem("loraT_done")
        loraT_ready = sem("loraT_ready")
        ffn_done = sem("ffn_done")
        result_ready = sem("result_ready")
        out_stored = [sem("out_stored0"), sem("out_stored1")]

        def ffn_bank(b):
            return tr_bank[b % 2] if b >= 6 else pj_bank[b % 2]

        block = ctx.enter_context(nc.Block())

        LAST = KV_HEADS - 1
        E = KV_HEADS
        TABLES = 5
        half = D // 2

        def cols(t):
            return slice(t * SEQ, (t + 1) * SEQ)

        def tok(b):
            return slice(b * P, (b + 1) * P)

        def split_keys(t):
            return slice(t * SEQ, (t + 1) * SEQ - P)

        def f32(ap):
            return ap.bitcast(F32)

        def groups(eng, body):
            body(0, True, False)
            with eng.Fori(1, LAST) as g:
                body(g, False, False)
            body(LAST, False, True)

        @block.sync
        def _(sp):
            def load_x(b):
                sp.dma_start(resid[:, b, :], x[b]).then_inc(x_in[b], 16)

            load_x(0)
            load_x(1)
            sp.dma_start(eye_sb[:, :], eye[:, :]).then_inc(eye_in, 16)
            load_x(2)
            load_x(3)
            sp.dma_start(wk_raw[:, :], wk[0]).then_inc(wk_in, 16)
            load_x(4)
            load_x(5)
            sp.dma_start(wv_raw[:, :], wv[0]).then_inc(wv_in, 16)
            sp.dma_start(wq_raw[:, 0, :], wq[0]).then_inc(wq_in[0], 16)
            sp.dma_start(cos_sb[:, :], cos_t[:, :]).then_inc(tables_in, 16)
            sp.dma_start(sin_sb[:, :], sin_t[:, :]).then_inc(tables_in, 16)
            load_x(6)
            load_x(7)
            sp.dma_start(wq_raw[:, 1, :], wq[1]).then_inc(wq_in[1], 16)
            sp.dma_start(band_sb[:, :], band[:, :]).then_inc(tables_in, 16)
            sp.dma_start(ag_sb[:, :], a_gate[:, :]).then_inc(tables_in, 16)
            sp.dma_start(bt_sb[:, :], b_thr[:, :]).then_inc(tables_in, 16)

            def loads(g, first, last):
                for j in range(PER_GROUP):
                    if not (last and j >= 2):
                        wait(sp, wq_lo_ready, g * PER_GROUP + (j + 1))
                        sp.dma_start(wq_raw[:, j % 2, :], wq[g * PER_GROUP + (j + 2)]).then_inc(wq_in[j % 2], 16)
                    if j == 0 and not last:
                        wait(sp, wk_lo_ready, g + 1)
                        sp.dma_start(wk_raw[:, :], wk[g + 1]).then_inc(wk_in, 16)
                    if j == 1 and not last:
                        wait(sp, wv_lo_ready, g + 1)
                        sp.dma_start(wv_raw[:, :], wv[g + 1]).then_inc(wv_in, 16)
                    if j >= 2:
                        for h in (2 * j - 4, 2 * j - 3):
                            wait(sp, wo_lo_ready, g * PER_GROUP + (h - 1))
                            sp.dma_start(wo_raw[:, h % 2, :], wo[g * PER_GROUP + h]).then_inc(wo_in[h % 2], 16)

            groups(sp, loads)

            sp.wait_ge(trans_done, trans_use(LAST, 3, 1, 1) + 1)
            sp.dma_start(wb_raw, w_base[:, :]).then_inc(wb_in, 16)
            sp.wait_ge(wk_lo_ready, KV_HEADS)
            sp.dma_start(bl_sb[:, :], b_lora[:, :]).then_inc(lora_bias_in, 16)
            sp.wait_ge(wv_lo_ready, KV_HEADS)
            sp.dma_start(bb_sb[:, :], b_base[:, :]).then_inc(lora_bias_in, 16)
            for b in range(BLOCKS):
                sp.wait_ge(result_ready, b + 1)
                sp.dma_start(out[b], result[:, b % 2, :]).then_inc(out_stored[b % 2], 16)
            for s in range(2):
                sp.wait_ge(out_stored[s], 16 * (BLOCKS // 2))

        @block.tensor
        def _(pe):
            def three(bank_cols, lhs, rhs, start, stop):
                nc.tensor.matmul(bank_cols, lhs[0], rhs[0], start=start, stop=False)
                nc.tensor.matmul(bank_cols, lhs[0], rhs[1], start=False, stop=False)
                return nc.tensor.matmul(bank_cols, lhs[1], rhs[0], start=False, stop=stop)

            def project(w_hi, w_lo, t, use, w_ready, w_count, in_bank=None):
                wait(pe, w_ready, w_count)
                wait(pe, proj_taken, use - 1)
                for c in range(KT):
                    w = slice(c * D, (c + 1) * D)
                    s = slice(t * SEQ, (t + 1) * SEQ)
                    mm = three(pj_bank[t if in_bank is None else in_bank % 2][:, :], (w_hi[:, w], w_lo[:, w]), (xT_hi[:, c, s], xT_lo[:, c, s]),
                               c == 0, c == KT - 1)
                mm.then_inc(proj_done, 1)

            def scores(g, j, p):
                t = p // 2
                wait(pe, q_lo_ready, g * 8 + (2 * j + t + 1))
                wait(pe, k_lo_ready, 2 * g + (t + 1))
                wait(pe, scores_masked, g * 16 + (4 * j + p - 1))
                for b in (2 * p, 2 * p + 1):
                    if b % QB == 0:
                        nc.tensor.matmul(sc_bank[p % 2][:, 0:P], rope_cos[:, t, 0:P], k_first[:, t, :],
                                         start=True, stop=True)
                        continue
                    q = slice(b * P, (b + 1) * P)
                    k = slice((b - 1) * P, (b + 1) * P)
                    mm = three(sc_bank[p % 2][:, (b % 2) * 2 * P:(b % 2 + 1) * 2 * P], (q_hi[:, q], q_lo[:, q]),
                               (k_hi[:, k], k_lo[:, k]), True, True)
                mm.then_inc(scores_done, 1)

            def transpose_probs(g, j, t):
                par = (j + 1) % 2
                wait(pe, (probs0_ready, probs1_ready)[t], g * PER_GROUP + j)
                for half in range(2):
                    use = trans_use(g, j, t, half)
                    wait(pe, trans_taken, use - 1)
                    parts = [(0, 0, 0), (1, 1, 0), (2, 1, P), (3, 2, 0)] if half == 0 else \
                            [(0, 3, P), (1, 2, P), (2, 3, 0)]
                    for slot, qb, col in parts:
                        mm = nc.tensor.transpose(tr_bank[half][:, slot * P:(slot + 1) * P],
                                                 probs[:, par, t * QB + qb, col:col + P], eye_sb[:, :])
                    mm.then_inc(trans_done, 1)

            def probs_v(g, j, t):
                use = pv_use(g, j, t)
                wait(pe, trans_taken, trans_use(g, j, t, 1) + 1)
                wait(pe, o_taken, use - 1)
                for i, (kb, slot) in enumerate(((0, 0), (2, 4), (1, 2))):
                    v = slice((t * QB + kb) * P, (t * QB + kb + 1) * P)
                    pc = slice(slot * P, (slot + 2) * P)
                    q0 = min(kb, QB - 2) * P
                    o = o_bank[t][:, q0:q0 + 2 * P]
                    for n, (a, b) in enumerate(((v_hi, pT_hi), (v_hi, pT_lo), (v_lo, pT_hi))):
                        nc.tensor.matmul(o, a[:, v], b[:, t, pc], start=(i == 0 and n == 0), stop=False,
                                         skip_group_check=True)
                mm = nc.tensor.matmul(o_bank[t][:, (QB - 1) * P:], v_last[:, t, :],
                                      pT_last[:, t, :], start=False, stop=True, skip_group_check=True)
                mm.then_inc(o_done, 1)

            def out_projection(g, b):
                use = out_use(g, b)
                wait(pe, wo_lo_ready, g * PER_GROUP)
                if b % QB == 0:
                    wait(pe, o_taken, pv_use(g, 0, b // QB) + 1)
                wait(pe, o_taken, use - 1)
                for h in range(PER_GROUP):
                    mm = three(o_bank[out_bank(g, b)][:, :], (oT_hi[:, h, tok(b)], oT_lo[:, h, tok(b)]),
                               (wo_hi[:, h, :], wo_lo[:, h, :]), h == 0, h == PER_GROUP - 1)
                mm.then_inc(o_done, 1)

            def transpose_v(g, t):
                use = v_trans_use(g, t)
                wait(pe, proj_taken, g * PROJ_PER_GROUP + PROJ_BEFORE)
                wait(pe, trans_taken, use - 1)
                for i in range(QB):
                    mm = nc.tensor.transpose(tr_bank[t][:, i * P:(i + 1) * P], vT[:, t, i * P:(i + 1) * P],
                                             eye_sb[:, :])
                mm.then_inc(trans_done, 1)

            pe.wait_ge(eye_in, 16)

            def transpose_x(b):
                pe.wait_ge(normed_ready, b + 1)
                wait(pe, xT_lo_ready, b - 1)
                for c in range(KT):
                    mm = nc.tensor.transpose(tr_bank[b % 2][:, tok(c)], normed[:, b % 4, tok(c)], eye_sb[:, :])
                mm.then_inc(xT_done, 1)

            def first_projection(use):
                t = use // 3
                w = ((wk_hi, wk_lo, wk_lo_ready), (wv_hi, wv_lo, wv_lo_ready), (wq_hi, wq_lo, wq_lo_ready))[use % 3]
                pe.wait_ge(xT_lo_ready, QB * (t + 1))
                project(w[0], w[1], t, use, w[2], 1, use)

            for b in range(QB):
                transpose_x(b)
            first_projection(0)
            transpose_x(4)
            transpose_x(5)
            first_projection(1)
            transpose_x(6)
            transpose_x(7)
            for use in range(2, PROJ_BEFORE):
                first_projection(use)

            def group_projection(g, j, t, last):
                if j == 2 and not last:
                    project(wk_hi, wk_lo, t, k_proj_use(g, t), wk_lo_ready, g + 2)
                if j == 3 and not last:
                    project(wv_hi, wv_lo, t, v_proj_use(g, t), wv_lo_ready, g + 2)

            def steps(g, first, last):
                for j in range(PER_GROUP):
                    before, after = not (first and j == 0), not (last and j == 3)
                    w_count = g * PER_GROUP + (j + 2)
                    scores(g, j, 0)
                    scores(g, j, 1)
                    if before:
                        transpose_probs(g, j, 0)
                    if after:
                        project(wq_hi, wq_lo, 0, q_proj_use(g, j, 0), wq_lo_ready, w_count)
                    scores(g, j, 2)
                    scores(g, j, 3)
                    if before:
                        transpose_probs(g, j, 1)
                    if j == 1:
                        wait(pe, trans_taken, v_trans_use(g, 1) + 1)
                    if before:
                        probs_v(g, j, 0)
                    if j == 1 and not first:
                        out_projection(g, 4)
                        out_projection(g, 5)
                    if after:
                        project(wq_hi, wq_lo, 1, q_proj_use(g, j, 1), wq_lo_ready, w_count)
                    if j == 1 and not first:
                        out_projection(g, 6)
                        out_projection(g, 7)
                    group_projection(g, j, 0, last)
                    if before:
                        probs_v(g, j, 1)
                    group_projection(g, j, 1, last)
                    if j == 0:
                        transpose_v(g, 0)
                        transpose_v(g, 1)
                        if not first:
                            for b in range(4):
                                out_projection(g, b)

            groups(pe, steps)
            for t in range(BATCH):
                transpose_probs(E, 0, t)
                probs_v(E, 0, t)

            def transpose_y(b):
                pe.wait_ge(y_normed, b + 1)
                if b >= 2:
                    pe.wait_ge(yT_lo_ready, b - 1)
                else:
                    pe.wait_ge(trans_taken, trans_use(E, 0, 1, 1) + 1)
                for c in range(KT):
                    mm = nc.tensor.transpose(tr_bank[b % 2][:, tok(c)], normed[:, b % 4, tok(c)], eye_sb[:, :])
                mm.then_inc(yT_done, 1)

            def down_and_gate(b):
                pe.wait_ge(yT_ready, b + 1)
                if b % QB == 0:
                    pe.wait_ge(scores_masked, 16 * KV_HEADS)
                    wait(pe, lora_scaled, b // QB)
                i = b % QB
                for c in range(KT):
                    mm = nc.tensor.matmul(sc_bank[i // 2][:, (i % 2) * GCOLS:(i % 2 + 1) * GCOLS],
                                          yT(b)[:, tok(c)], ag_sb[:, c * GCOLS:(c + 1) * GCOLS],
                                          start=c == 0, stop=c == KT - 1)
                mm.then_inc(down_done, 1)

            def transpose_lora(t):
                pe.wait_ge(lora_scaled, t + 1)
                if t == 0:
                    pe.wait_ge(o_taken, out_use(E, 6) + 1)
                else:
                    pe.wait_ge(loraT_ready, t)
                for i in range(QB):
                    mm = nc.tensor.transpose(o_bank[0][:, tok(i)], lora_h[:, i, :], eye_sb[:, :])
                mm.then_inc(loraT_done, 1)

            def base(b):
                pe.wait_ge(wb_lo_ready, KT)
                pe.wait_ge(yT_lo_ready, b + 1)
                if b < 6:
                    wait(pe, result_ready, b - 1)
                for c in range(KT):
                    w = slice(c % 2 * HIDDEN, (c % 2 + 1) * HIDDEN)
                    three(ffn_bank(b)[:, :], (xT_hi[:, c, tok(b)], xT_lo[:, c, tok(b)]),
                          (wb_hi[c // 2][:, w], wb_lo[c // 2][:, w]), c == 0, False)

            def lora(b):
                pe.wait_ge(loraT_ready, b // QB + 1)
                nc.tensor.matmul(ffn_bank(b)[:, :], lora_hT[:, b % QB, :], bl_sb[:, :], start=False,
                                 stop=True).then_inc(ffn_done, 1)

            for b in range(QB):
                out_projection(E, b)
            for i in range(QB):
                out_projection(E, QB + i)
                transpose_y(i)
                if i >= 2:
                    down_and_gate(i - 2)
            down_and_gate(2)
            down_and_gate(3)
            pe.wait_ge(proj_taken, q_proj_use(LAST, 2, 1) + 1)
            pe.wait_ge(lora_bias_in, 16 * 2)
            base(0)
            transpose_y(4)
            base(1)
            transpose_y(5)
            transpose_lora(0)
            lora(0)
            lora(1)
            transpose_y(6)
            base(2)
            lora(2)
            transpose_y(7)
            base(3)
            lora(3)
            for b in range(QB, BLOCKS):
                down_and_gate(b)
            for b in range(QB, BLOCKS):
                base(b)
            transpose_lora(1)
            for b in range(QB, BLOCKS):
                lora(b)

        @block.scalar
        def _(act):
            def copy(dst, src):
                return nc.scalar.activation(dst, src, ACT.Copy)

            def exp_pair(g, j, p):
                act.wait_ge(shift_ready, g * 16 + (4 * j + p + 1))
                for b in (2 * p, 2 * p + 1):
                    s = probs[:, j % 2, b, 0:P if b % QB == 0 else 2 * P]
                    last = nc.scalar.activation(s, s, ACT.Exp, bias=shift[:, j % 2, b:b + 1], scale=SM_SCALE,
                                                accum_out=row_sum[:, j % 2, b:b + 1])
                last.then_inc(exp_done, 1)

            def pT_split(g, j, t):
                wait(act, o_done, pv_use(g, j - 1, t) + 1 if j else pv_use(g - 1, 3, t) + 1)
                act.wait_ge(trans_done, trans_use(g, j, t, 0) + 1)
                copy(pT_hi[:, t, 0:4 * P], tr_bank[0][:, :]).then_inc(pT_hi_ready, 1)
                act.wait_ge(trans_done, trans_use(g, j, t, 1) + 1)
                copy(pT_hi[:, t, 4 * P:6 * P], tr_bank[1][:, P:3 * P]).then_inc(pT_hi_ready, 1)

            def swap(t, use, rope_use, bank_no=None):
                src = pj_bank[t if bank_no is None else bank_no]
                act.wait_ge(proj_done, use + 1)
                wait(act, rope_added, rope_use - 1)
                copy(rope_sin[0:half, t, :], src[half:D, :])
                copy(rope_sin[half:D, t, :], src[0:half, :]).then_inc(rope_swapped, 1)

            def k_swap(t, use, rope_use, bank_no=None):
                src = pj_bank[t if bank_no is None else bank_no]
                act.wait_ge(proj_done, use + 1)
                wait(act, k_added, rope_use - 1)
                copy(k_sin[0:half, t, :], src[half:D, :])
                copy(k_sin[half:D, t, :], src[0:half, :]).then_inc(k_swapped, 1)

            def k_split(t, count):
                act.wait_ge(k_added, count)
                copy(k_hi[:, cols(t)], k_rot[:, t, :]).then_inc(k_hi_ready, 1)

            def q_split(g, j, t):
                act.wait_ge(rope_added, q_rope_use(g, j, t) + 1)
                act.wait_ge(scores_done, g * 16 + (4 * j + 2 * t + 2))
                copy(q_hi[:, cols(t)], rope_cos[:, t, :]).then_inc(q_hi_ready, 1)

            def o_split(g, j, t):
                act.wait_ge(o_done, pv_use(g, j, t) + 1)
                copy(oT_hi[:, (j - 1) % PER_GROUP, cols(t)], o_bank[t][:, :]).then_inc(oT_hi_ready, 1)

            def x_split(b):
                act.wait_ge(xT_done, b + 1)
                copy(xT_hi[:, :, tok(b)], tr_bank[b % 2][:, :].rearrange("p (c n) -> p c n", c=KT))\
                    .then_inc(xT_hi_ready, 1)

            def first_q_split(t):
                act.wait_ge(rope_added, t + 1)
                copy(q_hi[:, cols(t)], rope_cos[:, t, :]).then_inc(q_hi_ready, 1)

            x_split(0)
            x_split(1)
            act.wait_ge(wk_in, 16)
            copy(wk_hi[:, :], wk_raw[:, :]).then_inc(wk_hi_ready, 1)
            x_split(2)
            x_split(3)
            act.wait_ge(wv_in, 16)
            copy(wv_hi[:, :], wv_raw[:, :]).then_inc(wv_hi_ready, 1)
            act.wait_ge(wq_in[0], 16)
            copy(wq_hi[:, :], wq_raw[:, 0, :]).then_inc(wq_hi_ready, 1)
            k_swap(0, 0, 0, 0)
            x_split(4)
            x_split(5)
            x_split(6)
            x_split(7)
            k_split(0, 1)
            swap(0, 2, 0, 0)
            first_q_split(0)
            k_swap(1, 3, 1, 1)
            k_split(1, 2)
            swap(1, 5, 1, 1)
            act.wait_ge(wq_in[1], 16)
            copy(wq_hi[:, :], wq_raw[:, 1, :]).then_inc(wq_hi_ready, 1)
            first_q_split(1)

            def steps(g, first, last):
                for j in range(PER_GROUP):
                    before, after = not (first and j == 0), not (last and j == 3)
                    exp_pair(g, j, 0)
                    if before:
                        pT_split(g, j, 0)
                    exp_pair(g, j, 1)
                    if after:
                        swap(0, q_proj_use(g, j, 0), q_rope_use(g, j, 0))
                    exp_pair(g, j, 2)
                    if before:
                        pT_split(g, j, 1)
                    exp_pair(g, j, 3)
                    if j == 3 and not last:
                        for t in range(BATCH):
                            act.wait_ge(scores_done, g * 16 + (12 + 2 * t + 2))
                            k_split(t, k_rope_use(g + 1, t) + 1)
                    if before:
                        o_split(g, j, 0)
                    if after:
                        q_split(g, j, 0)
                        swap(1, q_proj_use(g, j, 1), q_rope_use(g, j, 1))
                    if not (last and j >= 2):
                        act.wait_ge(wq_in[j % 2], (g * 2 + (j // 2 + 2)) * 16)
                        act.wait_ge(proj_done, q_proj_use(g, j, 1) + 1)
                        copy(wq_hi[:, :], wq_raw[:, j % 2, :]).then_inc(wq_hi_ready, 1)
                    if before:
                        o_split(g, j, 1)
                    if after:
                        q_split(g, j, 1)
                    if j == 2 and not last:
                        k_swap(0, k_proj_use(g, 0), k_rope_use(g + 1, 0))
                    if j == 0:
                        for t in range(BATCH):
                            act.wait_ge(trans_done, v_trans_use(g, t) + 1)
                            copy(v_last[:, t, :], tr_bank[t][:, 3 * P:])
                            copy(v_hi[:, split_keys(t)], tr_bank[t][:, 0:3 * P]).then_inc(v_hi_ready, 1)
                    if j == 0 and not last:
                        act.wait_ge(wk_in, (g + 2) * 16)
                        copy(wk_hi[:, :], wk_raw[:, :]).then_inc(wk_hi_ready, 1)
                    if j == 1 and not last:
                        act.wait_ge(wv_in, (g + 2) * 16)
                        copy(wv_hi[:, :], wv_raw[:, :]).then_inc(wv_hi_ready, 1)
                    if j >= 2:
                        for h in (2 * j - 4, 2 * j - 3):
                            act.wait_ge(wo_in[h % 2], (g * 2 + (h // 2 + 1)) * 16)
                            wait(act, o_done, out_use(g, 7) + 1)
                            copy(wo_hi[:, h, :], wo_raw[:, h % 2, :]).then_inc(wo_hi_ready, 1)
                    if j == 2 and not last:
                        k_swap(1, k_proj_use(g, 1), k_rope_use(g + 1, 1))

            groups(act, steps)
            for t in range(BATCH):
                pT_split(E, 0, t)
                o_split(E, 0, t)
            act.wait_ge(wb_in, 16)
            for n in range(2):
                copy(wb_hi[n][:, :], wb_raw[:, n * TOKENS:(n + 1) * TOKENS]).then_inc(wb_hi_ready, 1)

            def y_split(b):
                act.wait_ge(yT_done, b + 1)
                wait(act, down_done, b - 3)
                copy(yT(b), tr_bank[b % 2][:, :]).then_inc(yT_ready, 1)
                copy(xT_hi[:, :, tok(b)], tr_bank[b % 2][:, :].rearrange("p (c n) -> p c n", c=KT))\
                    .then_inc(yT_hi_ready, 1)

            def gate_exp(t):
                act.wait_ge(logits_ready, t + 1)
                nc.scalar.activation(gexp[:, :, :], logit[:, :, :], ACT.Exp).then_inc(gexp_done, 1)

            def lora_copy(t):
                act.wait_ge(loraT_done, t + 1)
                wait(act, ffn_done, QB * t)
                copy(lora_hT, o_bank[0][:, :].rearrange("p (a b) -> p a b", a=QB)).then_inc(loraT_ready, 1)

            for b in range(QB):
                y_split(b)
            gate_exp(0)
            y_split(4)
            y_split(5)
            lora_copy(0)
            y_split(6)
            y_split(7)
            gate_exp(1)
            lora_copy(1)

        @block.gpsimd
        def _(pool):
            nc.gpsimd.memset(minus_half[:, :], -0.5).then_inc(constant_set, 1)
            pool.wait_ge(constant_set, 1)

            def low(raw, hi, lo, hi_ready, count, lo_ready):
                pool.wait_ge(hi_ready, count)
                nc.gpsimd.tensor_tensor(lo, raw, hi.bitcast(F32), ALU.subtract).then_inc(lo_ready, 1)

            def wq_low(slot, count):
                low(wq_raw[:, slot, :], wq_hi[:, :], wq_lo[:, :], wq_hi_ready, count, wq_lo_ready)

            def block_rstd(b, count):
                pool.wait_ge(moments_ready, count)
                nc.gpsimd.tensor_scalar(var_eps[:, b:b + 1], moments[:, b, 1:2], EPS, None, ALU.add)\
                    .then_inc(var_ready, 1)
                pool.wait_ge(var_ready, count)
                nc.gpsimd.tensor_tensor(rstd[:, b:b + 1], var_eps[:, b:b + 1], minus_half[:, :], ALU.pow)\
                    .then_inc(rstd_ready, 1)

            for b in range(QB):
                block_rstd(b, b + 1)
            low(wk_raw[:, :], wk_hi[:, :], wk_lo[:, :], wk_hi_ready, 1, wk_lo_ready)
            block_rstd(4, 5)
            block_rstd(5, 6)
            low(wv_raw[:, :], wv_hi[:, :], wv_lo[:, :], wv_hi_ready, 1, wv_lo_ready)
            block_rstd(6, 7)
            block_rstd(7, 8)
            wq_low(0, 1)
            wq_low(1, 2)

            def k_low(t, count):
                pool.wait_ge(k_hi_ready, count)
                nc.gpsimd.tensor_tensor(k_lo[:, cols(t)], k_rot[:, t, :], f32(k_hi[:, cols(t)]), ALU.subtract)
                nc.gpsimd.tensor_copy(k_first[:, t, :], k_rot[:, t, 0:P]).then_inc(k_lo_ready, 1)

            for t in range(BATCH):
                k_low(t, t + 1)

            def k_rope(t, cos_use, rope_use):
                pool.wait_ge(k_swapped, rope_use + 1)
                nc.gpsimd.tensor_tensor(k_sin[:, t, :], k_sin[:, t, :], sin_sb[:, :], ALU.mult).then_inc(k_scaled, 1)
                pool.wait_ge(k_scaled, rope_use + 1)
                pool.wait_ge(proj_taken, cos_use + 1)
                nc.gpsimd.tensor_tensor(k_rot[:, t, :], k_rot[:, t, :], k_sin[:, t, :], ALU.add).then_inc(k_added, 1)

            def normalise(g, j, t):
                pool.wait_ge(inv_ready, g * 8 + (2 * j + t + 1))
                b = t * QB
                s = probs[:, j % 2, b, 0:P]
                nc.gpsimd.tensor_tensor(s, s, inv_sum[:, j % 2, b:b + 1].to_broadcast([P, P]), ALU.mult)
                s = probs[:, j % 2, b + 1:b + QB, :]
                inv = inv_sum[:, j % 2, b + 1:b + QB].unsqueeze(2).to_broadcast([P, QB - 1, 2 * P])
                nc.gpsimd.tensor_tensor(s, s, inv, ALU.mult).then_inc(probs1_ready, 1)

            def steps(g, first, last):
                for j in range(PER_GROUP):
                    if j == 3 and not last:
                        for t in range(BATCH):
                            k_rope(t, k_proj_use(g, t), k_rope_use(g + 1, t))
                        for t in range(BATCH):
                            k_low(t, 2 * g + (t + 3))
                    if not (last and j >= 2):
                        wq_low(j % 2, g * PER_GROUP + (j + 3))
                    normalise(g, j, 1)
                    if j == 0 and not last:
                        low(wk_raw[:, :], wk_hi[:, :], wk_lo[:, :], wk_hi_ready, g + 2, wk_lo_ready)
                    if j == 1 and not last:
                        low(wv_raw[:, :], wv_hi[:, :], wv_lo[:, :], wv_hi_ready, g + 2, wv_lo_ready)
                    if j >= 2:
                        for h in (2 * j - 4, 2 * j - 3):
                            low(wo_raw[:, h % 2, :], wo_hi[:, h, :], wo_lo[:, h, :], wo_hi_ready,
                                g * PER_GROUP + (h + 1), wo_lo_ready)

            groups(pool, steps)
            for b in range(BLOCKS):
                block_rstd(b, BLOCKS + b + 1)
                if b < KT:
                    w = slice(b * HIDDEN, (b + 1) * HIDDEN)
                    part = slice(b % 2 * HIDDEN, (b % 2 + 1) * HIDDEN)
                    low(wb_raw[:, w], wb_hi[b // 2][:, part], wb_lo[b // 2][:, part], wb_hi_ready, b // 2 + 1,
                        wb_lo_ready)
            pool.wait_ge(lora_bias_in, 16 * 2)
            for b in range(BLOCKS):
                pool.wait_ge(y_normed, b + 1)
                nc.gpsimd.tensor_tensor(resid[:, b, :], resid[:, b, :], bb_sb[:, :], ALU.add)\
                    .then_inc(bias_added, 1)

        @block.vector
        def _(dve):
            TT = nc.vector.tensor_tensor

            def mask_pair(g, j, p):
                dve.wait_ge(scores_done, g * 16 + (4 * j + p + 1))
                nc.vector.memset(gap[:, :], 0.0)
                for b in (2 * p, 2 * p + 1):
                    w = P if b % QB == 0 else 2 * P
                    c0 = (b % 2) * 2 * P
                    last = nc.vector.tensor_tensor_reduce(
                        out=probs[:, j % 2, b, 0:w], in0=sc_bank[p % 2][:, c0:c0 + w],
                        in1=band_sb[:, 2 * P - w:2 * P], scale=1.0, scalar=LOWEST, op0=ALU.add, op1=ALU.max,
                        accum_out=row_max[:, j % 2, b:b + 1])
                last.then_inc(scores_masked, 1)

            def shift_pair(g, j, p):
                n = g * 16 + (4 * j + p + 1)
                dve.wait_ge(scores_masked, n)
                nc.vector.tensor_scalar(shift[:, j % 2, 2 * p:2 * p + 2], row_max[:, j % 2, 2 * p:2 * p + 2],
                                        -SM_SCALE, None, ALU.mult).then_inc(shift_ready, 1)

            def normalise(g, j, t):
                n = g * 8 + (2 * j + t + 1)
                dve.wait_ge(exp_done, g * 16 + (4 * j + 2 * t + 2))
                bs = slice(t * QB, (t + 1) * QB)
                nc.vector.reciprocal(inv_sum[:, j % 2, bs], row_sum[:, j % 2, bs]).then_inc(inv_ready, 1)
                if t:
                    return
                dve.wait_ge(inv_ready, n)
                for b in range(t * QB, (t + 1) * QB):
                    s = probs[:, j % 2, b, 0:P if b % QB == 0 else 2 * P]
                    last = nc.vector.tensor_scalar(s, s, inv_sum[:, j % 2, b:b + 1], None, ALU.mult)
                last.then_inc(probs0_ready, 1)

            def pT_low(g, j, t):
                n = g * 16 + (4 * j - 4 + 2 * t + 1)
                dve.wait_ge(pT_hi_ready, n)
                c = slice(0, 4 * P)
                TT(pT_lo[:, t, c], tr_bank[0][:, :], f32(pT_hi[:, t, c]), ALU.subtract).then_inc(trans_taken, 1)
                dve.wait_ge(pT_hi_ready, n + 1)
                nc.vector.tensor_copy(pT_last[:, t, :], tr_bank[1][:, 0:P])
                c = slice(4 * P, 6 * P)
                TT(pT_lo[:, t, c], tr_bank[1][:, P:3 * P], f32(pT_hi[:, t, c]), ALU.subtract)\
                    .then_inc(trans_taken, 1)

            def rope(dst, t, use, rope_use, bank_no=None):
                dve.wait_ge(rope_swapped, rope_use + 1)
                TT(dst[:, t, :], pj_bank[t if bank_no is None else bank_no][:, :], cos_sb[:, :], ALU.mult).then_inc(proj_taken, 1)
                TT(rope_sin[:, t, :], rope_sin[:, t, :], sin_sb[:, :], ALU.mult).then_inc(rope_scaled, 1)

            def k_cos(t, rope_use, bank_no=None):
                dve.wait_ge(k_swapped, rope_use + 1)
                TT(k_rot[:, t, :], pj_bank[t if bank_no is None else bank_no][:, :], cos_sb[:, :], ALU.mult)\
                    .then_inc(proj_taken, 1)

            def first_k_rope(t, use):
                k_cos(t, t, use % 2)
                TT(k_sin[:, t, :], k_sin[:, t, :], sin_sb[:, :], ALU.mult).then_inc(k_scaled, 1)
                dve.wait_ge(proj_taken, use + 1)
                dve.wait_ge(k_scaled, t + 1)
                TT(k_rot[:, t, :], k_rot[:, t, :], k_sin[:, t, :], ALU.add).then_inc(k_added, 1)

            def rope_add(dst, t, use, rope_use):
                dve.wait_ge(proj_taken, use + 1)
                dve.wait_ge(rope_scaled, rope_use + 1)
                TT(dst[:, t, :], dst[:, t, :], rope_sin[:, t, :], ALU.add).then_inc(rope_added, 1)

            def q_low(count, t):
                dve.wait_ge(q_hi_ready, count)
                TT(q_lo[:, cols(t)], rope_cos[:, t, :], f32(q_hi[:, cols(t)]), ALU.subtract).then_inc(q_lo_ready, 1)

            def o_low(g, j, t):
                dve.wait_ge(oT_hi_ready, g * 8 + (2 * j - 2 + t + 1))
                h = (j - 1) % PER_GROUP
                TT(oT_lo[:, h, cols(t)], o_bank[t][:, :], f32(oT_hi[:, h, cols(t)]), ALU.subtract)\
                    .then_inc(o_taken, 1)

            def add_out(g, b):
                dve.wait_ge(o_done, out_use(g, b) + 1)
                TT(resid[:, b, :], o_bank[out_bank(g, b)][:, :], resid[:, b, :], ALU.add).then_inc(o_taken, 1)

            def v_copy(t, use, bank_no=None):
                dve.wait_ge(proj_done, use + 1)
                nc.vector.tensor_copy(vT[:, t, :], pj_bank[t if bank_no is None else bank_no][:, :]).then_inc(proj_taken, 1)

            lns = [0]

            def chain(ins):
                lns[0] += 1
                ins.then_inc(ln_step, 1)
                dve.wait_ge(ln_step, lns[0])

            def block_moments(b):
                chain(nc.vector.bn_stats(stats[:, b, :], resid[:, b, :]))
                nc.vector.bn_aggr(moments[:, b, :], stats[:, b, :]).then_inc(moments_ready, 1)

            def normalise_block(b, count, free, ready):
                dve.wait_ge(rstd_ready, count)
                wait(dve, free, b - 3)
                nc.vector.tensor_scalar(normed[:, b % 4, :], resid[:, b, :], moments[:, b, 0:1], rstd[:, b:b + 1],
                                        ALU.subtract, ALU.mult).then_inc(ready, 1)

            def xT_low(b, hi_ready, lo_ready):
                dve.wait_ge(hi_ready, b + 1)
                TT(xT_lo[:, :, tok(b)], tr_bank[b % 2][:, :].rearrange("p (c n) -> p c n", c=KT),
                   f32(xT_hi[:, :, tok(b)]), ALU.subtract).then_inc(lo_ready, 1)

            def load_moments(b):
                dve.wait_ge(x_in[b], 16)
                block_moments(b)

            def normalise_x(b):
                normalise_block(b, b + 1, xT_done, normed_ready)

            def split_x(b):
                xT_low(b, xT_hi_ready, xT_lo_ready)

            load_moments(0)
            load_moments(1)
            normalise_x(0)
            load_moments(2)
            normalise_x(1)
            load_moments(3)
            normalise_x(2)
            split_x(0)
            normalise_x(3)
            split_x(1)
            split_x(2)
            split_x(3)
            for b in (4, 5):
                load_moments(b)
            for b in (4, 5):
                normalise_x(b)
            dve.wait_ge(tables_in, 16 * TABLES)
            first_k_rope(0, 0)
            split_x(4)
            for b in (6, 7):
                load_moments(b)
            split_x(5)
            for b in (6, 7):
                normalise_x(b)
            v_copy(0, 1, 1)
            split_x(6)
            split_x(7)
            rope(rope_cos, 0, 2, 0, 0)
            rope_add(rope_cos, 0, 2, 0)
            first_k_rope(1, 3)
            q_low(1, 0)
            v_copy(1, 4, 0)
            rope(rope_cos, 1, 5, 1, 1)
            rope_add(rope_cos, 1, 5, 1)
            q_low(2, 1)

            def steps(g, first, last):
                for j in range(PER_GROUP):
                    before, after = not (first and j == 0), not (last and j == 3)
                    use = [q_proj_use(g, j, t) for t in range(BATCH)]
                    rot = [q_rope_use(g, j, t) for t in range(BATCH)]
                    mask_pair(g, j, 0)
                    shift_pair(g, j, 0)
                    mask_pair(g, j, 1)
                    shift_pair(g, j, 1)
                    if j == 3 and not last:
                        k_cos(1, k_rope_use(g + 1, 1))
                    if before:
                        pT_low(g, j, 0)
                    normalise(g, j, 0)
                    mask_pair(g, j, 2)
                    shift_pair(g, j, 2)
                    mask_pair(g, j, 3)
                    shift_pair(g, j, 3)
                    if after:
                        rope(rope_cos, 0, use[0], rot[0])
                    if before:
                        pT_low(g, j, 1)
                    if after:
                        rope_add(rope_cos, 0, use[0], rot[0])
                    if before:
                        o_low(g, j, 0)
                    if j == 1 and not first:
                        add_out(g, 4)
                        add_out(g, 5)
                    if after:
                        q_low(g * 8 + (2 * j + 3), 0)
                        rope(rope_cos, 1, use[1], rot[1])
                        rope_add(rope_cos, 1, use[1], rot[1])
                    if j == 1 and not first:
                        add_out(g, 6)
                        add_out(g, 7)
                    if before:
                        o_low(g, j, 1)
                    normalise(g, j, 1)
                    if after:
                        q_low(g * 8 + (2 * j + 4), 1)
                    if j == 0:
                        for t in range(BATCH):
                            dve.wait_ge(v_hi_ready, 2 * g + (t + 1))
                            keys = split_keys(t)
                            TT(v_lo[:, keys], tr_bank[t][:, 0:3 * P], f32(v_hi[:, keys]), ALU.subtract)\
                                .then_inc(trans_taken, 1)
                        if not first:
                            for b in range(QB):
                                add_out(g, b)
                    if j == 2 and not last:
                        k_cos(0, k_rope_use(g + 1, 0))
                    if j == 3 and not last:
                        for t in range(BATCH):
                            v_copy(t, v_proj_use(g, t))

            groups(dve, steps)
            for t in range(BATCH):
                pT_low(E, 0, t)
                o_low(E, 0, t)

            def gates(t):
                dve.wait_ge(down_done, QB * (t + 1))
                for k in range(2):
                    v = sc_bank[k][:, 0:2 * GCOLS].rearrange("p (a b) -> p a b", a=2)
                    last = nc.vector.tensor_copy(logit[:, 2 * k:2 * k + 2, :], v[:, :, ER:GCOLS])
                chain(last)
                z = logit[:, :, EXPERTS]
                chain(nc.vector.tensor_reduce(gmax[:, :], logit[:, :, 0:EXPERTS], AX.X, ALU.max))
                nc.vector.tensor_scalar(z, z, bt_sb[:, 0:1], -1.0, ALU.add, ALU.mult)
                TT(logit[:, :, 0:EXPERTS], logit[:, :, 0:EXPERTS], gmax[:, :].unsqueeze(2).to_broadcast([P, QB, EXPERTS]),
                   ALU.subtract).then_inc(logits_ready, 1)
                dve.wait_ge(gexp_done, t + 1)
                e = gexp[:, :, 0:EXPERTS]
                chain(nc.vector.tensor_reduce(gsum[:, :], e, AX.X, ALU.add))
                chain(nc.vector.reciprocal(ginv[:, :], gsum[:, :]))
                chain(nc.vector.tensor_scalar(thr[:, :], gexp[:, :, EXPERTS], 1.0, None, ALU.add))
                chain(nc.vector.reciprocal(thr[:, :], thr[:, :]))
                chain(nc.vector.tensor_scalar(thr[:, :], thr[:, :], MAX_THRESHOLD, None, ALU.mult))

                def wide(a):
                    return a[:, :].unsqueeze(2).to_broadcast([P, QB, EXPERTS])

                chain(TT(gate[:, :, :], e, wide(ginv), ALU.mult))
                chain(TT(gate[:, :, :], gate[:, :, :], wide(thr), ALU.subtract))
                chain(nc.vector.tensor_scalar(gate[:, :, :], gate[:, :, :], 0.0, None, ALU.max))
                chain(nc.vector.tensor_reduce(gsum[:, :], gate[:, :, :], AX.X, ALU.add))
                chain(nc.vector.tensor_scalar(iszero[:, :], gsum[:, :], 0.0, None, ALU.is_equal))
                chain(TT(gsum[:, :], gsum[:, :], iszero[:, :], ALU.add))
                chain(nc.vector.reciprocal(ginv[:, :], gsum[:, :]))
                chain(nc.vector.tensor_scalar(ginv[:, :], ginv[:, :], LORA_SCALING, None, ALU.mult))
                chain(TT(gate[:, :, :], gate[:, :, :], wide(ginv), ALU.mult))
                wait(dve, loraT_done, t)
                for i in range(QB):
                    c0 = (i % 2) * GCOLS
                    last = TT(lora_h[:, i, :].rearrange("p (e r) -> p e r", e=EXPERTS),
                              sc_bank[i // 2][:, c0:c0 + ER].rearrange("p (e r) -> p e r", e=EXPERTS),
                              gate[:, i, :].unsqueeze(2).to_broadcast([P, EXPERTS, RANK]), ALU.mult)
                last.then_inc(lora_scaled, 1)

            def finish(b):
                dve.wait_ge(ffn_done, b + 1)
                dve.wait_ge(bias_added, b + 1)
                if b >= 2:
                    dve.wait_ge(out_stored[b % 2], 16 * (b // 2))
                TT(result[:, b % 2, :], ffn_bank(b)[:, :], resid[:, b, :], ALU.add).then_inc(result_ready, 1)

            for b in range(QB):
                add_out(E, b)
                dve.wait_ge(o_taken, out_use(E, b) + 1)
                block_moments(b)
            for b in range(QB):
                normalise_block(b, BLOCKS + b + 1, yT_done, y_normed)
                add_out(E, QB + b)
                dve.wait_ge(o_taken, out_use(E, QB + b) + 1)
                block_moments(QB + b)
                xT_low(b, yT_hi_ready, yT_lo_ready)
            for b in (4, 5):
                normalise_block(b, BLOCKS + b + 1, yT_done, y_normed)
            gates(0)
            xT_low(4, yT_hi_ready, yT_lo_ready)
            normalise_block(6, BLOCKS + 7, yT_done, y_normed)
            xT_low(5, yT_hi_ready, yT_lo_ready)
            normalise_block(7, BLOCKS + 8, yT_done, y_normed)
            finish(0)
            finish(1)
            xT_low(6, yT_hi_ready, yT_lo_ready)
            finish(2)
            xT_low(7, yT_hi_ready, yT_lo_ready)
            finish(3)
            gates(1)
            for b in range(QB, BLOCKS):
                finish(b)


def kernel(L0_attn_x, L0_attn_wq, L0_attn_wk, L0_attn_wv, L0_attn_wo, L0_ffn_W_base, L0_ffn_b_base, L0_ffn_W_gate,
           L0_ffn_W_thr, L0_ffn_b_thr, L0_ffn_A_w, L0_ffn_B_w):
    import concourse.bacc as bacc
    from concourse.bass_utils import run_bass_kernel_spmd

    def lay(a):
        return np.ascontiguousarray(a)

    def heads_first(w, heads):
        return lay(np.asarray(w).reshape(KT, P, heads, D).transpose(2, 1, 0, 3).reshape(heads, P, KT * D))

    def channel_tiles(w):
        w = np.asarray(w)
        return lay(w.reshape(KT, P, w.shape[1]).transpose(1, 0, 2).reshape(P, KT * w.shape[1]))

    inv_freq = np.float32(10000.0) ** (-np.arange(D // 2, dtype=np.float32) / np.float32(D // 2))
    angle = inv_freq.astype(np.float32)[:, None] * np.arange(SEQ, dtype=np.float32)[None, :]
    cos_t = np.concatenate([np.cos(angle), np.cos(angle)]).astype(np.float32)
    sin_t = np.concatenate([-np.sin(angle), np.sin(angle)]).astype(np.float32)
    i, jj = np.arange(P)[:, None], np.arange(P)[None, :]
    band = np.concatenate([np.where(jj > i, 0.0, MASKED), np.where(jj <= i, 0.0, MASKED)], axis=1).astype(np.float32)

    a_w = np.asarray(L0_ffn_A_w).reshape(ER, HIDDEN)
    a_gate = np.concatenate([a_w, np.asarray(L0_ffn_W_gate), np.asarray(L0_ffn_W_thr)[None, :]]).T
    ins = {
        "x": lay(np.asarray(L0_attn_x).reshape(BLOCKS, P, HIDDEN)),
        "wq": heads_first(L0_attn_wq, HEADS),
        "wk": heads_first(L0_attn_wk, KV_HEADS),
        "wv": heads_first(L0_attn_wv, KV_HEADS),
        "wo": lay(np.asarray(L0_attn_wo).reshape(HEADS, D, HIDDEN)),
        "w_base": channel_tiles(np.asarray(L0_ffn_W_base).T),
        "b_base": lay(np.broadcast_to(np.asarray(L0_ffn_b_base)[None, :], (P, HIDDEN))),
        "a_gate": channel_tiles(a_gate),
        "b_thr": lay(np.broadcast_to(np.asarray(L0_ffn_b_thr)[None, :], (P, 1))),
        "b_lora": lay(np.asarray(L0_ffn_B_w).transpose(0, 2, 1).reshape(ER, HIDDEN)),
        "cos_t": cos_t,
        "sin_t": sin_t,
        "band": band,
        "eye": np.eye(P, dtype=np.float32),
    }
    nc = bacc.Bacc("TRN2", target_bir_lowering=False, num_devices=1)
    arrays, args = {}, []
    for name, a in ins.items():
        arrays[f"in_{name}"] = a
        args.append(nc.dram_tensor(f"in_{name}", a.shape, F32, kind="ExternalInput").ap())
    res = nc.dram_tensor("layer_out", (BLOCKS, P, HIDDEN), F32, kind="ExternalOutput").ap()
    layer_kernel(nc, *args, res)
    r = run_bass_kernel_spmd(nc, [arrays], core_ids=[0])
    return r.results[0]["layer_out"].reshape(BATCH, SEQ, HIDDEN)
```

```python
import numpy as np
import concourse.bass as bass
from concourse import mybir
from contextlib import ExitStack

F32 = mybir.dt.float32
F32R = mybir.dt.float32r
ALU = mybir.AluOpType
ACT = mybir.ActivationFunctionType
AX = mybir.AxisListType

BATCH, SEQ, HIDDEN = 2, 512, 512
HEADS, KV_HEADS, D = 32, 8, 128
PER_GROUP = HEADS // KV_HEADS
TOKENS = BATCH * SEQ
P = 128
KT = HIDDEN // P
QB = SEQ // P
BLOCKS = TOKENS // P
SM_SCALE = float(D) ** -0.5
MASKED = -1.0e38
LOWEST = -3.4e38
EPS = 1e-5
EXPERTS, RANK = 8, 16
ER = EXPERTS * RANK
GCOLS = ER + EXPERTS + 1
LORA_SCALING = 2.0
MAX_THRESHOLD = 0.125

PROJ_BEFORE = 6
PROJ_PER_GROUP = 12


def is_group(g, n):
    return isinstance(g, int) and g == n


def q_proj_use(g, j, t):
    return g * PROJ_PER_GROUP + (PROJ_BEFORE + (0, 2, 4, 8)[j] + t)


def k_proj_use(g, t):
    return g * PROJ_PER_GROUP + (PROJ_BEFORE + 6 + t)


def v_proj_use(g, t):
    return g * PROJ_PER_GROUP + (PROJ_BEFORE + 10 + t)


def q_rope_use(g, j, t):
    return g * 8 + (2 * j + t + 2)


def k_rope_use(g, t):
    return 2 * g + t


def trans_use(g, j, t, half):
    return g * 18 + (4 * j - 4 + (2 if j else 0) + 2 * t + half)


def v_trans_use(g, t):
    return g * 18 + t


def pv_use(g, j, t):
    if j == 1 and t == 0:
        return 0 if is_group(g, 0) else g * 16 - 4
    return g * 16 + ((-10, 0, 2, 4)[j] + t)


def out_use(g, b):
    behind = is_group(g, KV_HEADS)
    return g * 16 + (b - 8 + (b >= QB and not behind))


def out_bank(g, b):
    behind = is_group(g, KV_HEADS)
    return (b + (b >= QB and not behind)) % 2


def wait(eng, sem, count):
    if isinstance(count, int) and count <= 0:
        return
    eng.wait_ge(sem, count)


def layer_kernel(nc, x, wq, wk, wv, wo, w_base, b_base, a_gate, b_thr, b_lora, cos_t, sin_t, band, eye, out):
    ctx = ExitStack()
    with ctx:
        def sb(name, shape, dt=F32):
            return ctx.enter_context(nc.sbuf_tensor(name, shape, dt))

        def bank(name):
            return ctx.enter_context(nc.psum_tensor(name, [P, 512], F32))

        def sem(name):
            return ctx.enter_context(nc.semaphore(name))

        resid = sb("resid", [P, BLOCKS, HIDDEN])
        xT_hi = sb("xT_hi", [P, KT, TOKENS], F32R)
        xT_lo = sb("xT_lo", [P, KT, TOKENS], F32R)
        wq_raw = sb("wq_raw", [P, 2, KT * D])
        wk_raw = sb("wk_raw", [P, KT * D])
        wv_raw = sb("wv_raw", [P, KT * D])
        wo_raw = sb("wo_raw", [P, 2, HIDDEN])
        wq_hi = sb("wq_hi", [P, KT * D], F32R)
        wq_lo = sb("wq_lo", [P, KT * D], F32R)
        wk_hi = sb("wk_hi", [P, KT * D], F32R)
        wk_lo = sb("wk_lo", [P, KT * D], F32R)
        wv_hi = sb("wv_hi", [P, KT * D], F32R)
        wv_lo = sb("wv_lo", [P, KT * D], F32R)
        wo_hi = sb("wo_hi", [P, PER_GROUP, HIDDEN], F32R)
        wo_lo = sb("wo_lo", [P, PER_GROUP, HIDDEN], F32R)
        q_hi = sb("q_hi", [P, TOKENS], F32R)
        q_lo = sb("q_lo", [P, TOKENS], F32R)
        k_hi = sb("k_hi", [P, TOKENS], F32R)
        k_lo = sb("k_lo", [P, TOKENS], F32R)
        v_hi = sb("v_hi", [P, TOKENS], F32R)
        v_lo = sb("v_lo", [P, TOKENS], F32R)
        rope_cos = sb("rope_cos", [P, BATCH, SEQ])
        rope_sin = sb("rope_sin", [P, BATCH, SEQ])
        k_rot = sb("k_rot", [P, BATCH, SEQ])
        k_sin = sb("k_sin", [P, BATCH, SEQ])
        k_first = sb("k_first", [P, BATCH, P])
        vT = sb("vT", [P, BATCH, SEQ])
        probs = sb("probs", [P, 2, BLOCKS, 2 * P])
        pT_hi = sb("pT_hi", [P, BATCH, 6 * P], F32R)
        pT_lo = sb("pT_lo", [P, BATCH, 6 * P], F32R)
        oT_hi = sb("oT_hi", [P, PER_GROUP, TOKENS], F32R)
        oT_lo = sb("oT_lo", [P, PER_GROUP, TOKENS], F32R)
        v_last = sb("v_last", [P, BATCH, P])
        pT_last = sb("pT_last", [P, BATCH, P])
        cos_sb = sb("cos_sb", [P, SEQ])
        sin_sb = sb("sin_sb", [P, SEQ])
        band_sb = sb("band_sb", [P, 2 * P])
        eye_sb = sb("eye_sb", [P, P])
        row_max = sb("row_max", [P, 2, BLOCKS])
        shift = sb("shift", [P, 2, BLOCKS])
        row_sum = sb("row_sum", [P, 2, BLOCKS])
        inv_sum = sb("inv_sum", [P, 2, BLOCKS])
        stats = sb("stats", [P, BLOCKS, 6])
        moments = sb("moments", [P, BLOCKS, 2])
        rstd = sb("rstd", [P, BLOCKS])
        var_eps = sb("var_eps", [P, BLOCKS])
        gap = sb("gap", [P, 1])
        minus_half = sb("minus_half", [P, 1])
        wb_raw = probs[:, 0, :, :].rearrange("p a b -> p (a b)")
        wb_hi = (k_hi, q_hi)
        wb_lo = (k_lo, q_lo)
        normed = probs[:, 1, :, :].rearrange("p (s a) b -> p s (a b)", s=4)

        def yT(b):
            return (rope_sin if b % 4 < 2 else rope_cos)[:, b % 2, :]

        result = k_rot
        lora_h = vT[:, 0, :].rearrange("p (a b) -> p a b", a=QB)
        lora_hT = vT[:, 1, :].rearrange("p (a b) -> p a b", a=QB)
        ag_sb = sb("ag_sb", [P, KT * GCOLS])
        bl_sb = wk_raw
        bb_sb = wv_raw
        bt_sb = sb("bt_sb", [P, 1])
        logit = sb("logit", [P, QB, EXPERTS + 1])
        gmax = sb("gmax", [P, QB])
        gexp = sb("gexp", [P, QB, EXPERTS + 1])
        gate = sb("gate", [P, QB, EXPERTS])
        gsum = sb("gsum", [P, QB])
        ginv = sb("ginv", [P, QB])
        thr = sb("thr", [P, QB])
        iszero = sb("iszero", [P, QB])

        sc_bank = [bank("sc0"), bank("sc1")]
        pj_bank = [bank("pj0"), bank("pj1")]
        tr_bank = [bank("tr0"), bank("tr1")]
        o_bank = [bank("ob0"), bank("ob1")]
        x_bank = tr_bank + o_bank

        x_in = [sem(f"x_in{b}") for b in range(BLOCKS)]
        eye_in = sem("eye_in")
        rope_tables_in = sem("rope_tables_in")
        tables_in = sem("tables_in")
        wq_in = [sem("wq_in0"), sem("wq_in1")]
        wk_in = sem("wk_in")
        wv_in = sem("wv_in")
        wo_in = [sem("wo_in0"), sem("wo_in1")]
        wq_hi_ready = sem("wq_hi_ready")
        wq_lo_ready = sem("wq_lo_ready")
        wk_hi_ready = sem("wk_hi_ready")
        wk_lo_ready = sem("wk_lo_ready")
        wv_hi_ready = sem("wv_hi_ready")
        wv_lo_ready = sem("wv_lo_ready")
        wo_hi_ready = sem("wo_hi_ready")
        wo_lo_ready = sem("wo_lo_ready")
        ln_step = sem("ln_step")
        moments_ready = sem("moments_ready")
        var_ready = sem("var_ready")
        rstd_ready = sem("rstd_ready")
        normed_ready = sem("normed_ready")
        xT_done = sem("xT_done")
        xT_hi_ready = sem("xT_hi_ready")
        xT_lo_ready = sem("xT_lo_ready")
        proj_done = sem("proj_done")
        proj_taken = sem("proj_taken")
        rope_swapped = sem("rope_swapped")
        rope_scaled = sem("rope_scaled")
        rope_added = sem("rope_added")
        k_swapped = sem("k_swapped")
        k_scaled = sem("k_scaled")
        k_added = sem("k_added")
        q_hi_ready = sem("q_hi_ready")
        q_lo_ready = sem("q_lo_ready")
        k_hi_ready = sem("k_hi_ready")
        k_lo_ready = sem("k_lo_ready")
        v_hi_ready = sem("v_hi_ready")
        scores_done = sem("scores_done")
        scores_masked = sem("scores_masked")
        shift_ready = sem("shift_ready")
        exp_done = sem("exp_done")
        inv_ready = sem("inv_ready")
        probs0_ready = sem("probs0_ready")
        probs1_ready = sem("probs1_ready")
        trans_done = sem("trans_done")
        pT_hi_ready = sem("pT_hi_ready")
        trans_taken = sem("trans_taken")
        o_done = sem("o_done")
        oT_hi_ready = sem("oT_hi_ready")
        o_taken = sem("o_taken")
        constant_set = sem("constant_set")
        wb_in = sem("wb_in")
        lora_bias_in = sem("lora_bias_in")
        wb_hi_ready = sem("wb_hi_ready")
        wb_lo_ready = sem("wb_lo_ready")
        y_normed = sem("y_normed")
        yT_done = sem("yT_done")
        yT_ready = sem("yT_ready")
        yT_hi_ready = sem("yT_hi_ready")
        yT_lo_ready = sem("yT_lo_ready")
        bias_added = sem("bias_added")
        down_done = sem("down_done")
        logits_ready = sem("logits_ready")
        gexp_done = sem("gexp_done")
        lora_scaled = sem("lora_scaled")
        loraT_done = sem("loraT_done")
        loraT_ready = sem("loraT_ready")
        ffn_done = sem("ffn_done")
        result_ready = sem("result_ready")
        out_stored = [sem("out_stored0"), sem("out_stored1")]

        def proj_bank(t, in_bank):
            return pj_bank[t if in_bank is None else in_bank]

        def last_bank(b):
            return (pj_bank + sc_bank)[b] if b < QB else o_bank[b % 2]

        def ffn_bank(b):
            return tr_bank[b % 2] if b >= 6 else pj_bank[b % 2]

        block = ctx.enter_context(nc.Block())

        LAST = KV_HEADS - 1
        E = KV_HEADS
        TABLES = 3
        half = D // 2

        def cols(t):
            return slice(t * SEQ, (t + 1) * SEQ)

        def tok(b):
            return slice(b * P, (b + 1) * P)

        def split_keys(t):
            return slice(t * SEQ, (t + 1) * SEQ - P)

        def f32(ap):
            return ap.bitcast(F32)

        def groups(eng, body):
            body(0, True, False)
            with eng.Fori(1, LAST) as g:
                body(g, False, False)
            body(LAST, False, True)

        @block.sync
        def _(sp):
            def load_x(b):
                sp.dma_start(resid[:, b, :], x[b]).then_inc(x_in[b], 16)

            load_x(0)
            load_x(1)
            sp.dma_start(eye_sb[:, :], eye[:, :]).then_inc(eye_in, 16)
            load_x(2)
            load_x(3)
            sp.dma_start(wk_raw[:, :], wk[0]).then_inc(wk_in, 16)
            sp.dma_start(wq_raw[:, 0, :], wq[0]).then_inc(wq_in[0], 16)
            for b in range(QB, BLOCKS):
                load_x(b)
            sp.dma_start(cos_sb[:, :], cos_t[:, :]).then_inc(rope_tables_in, 16)
            sp.dma_start(sin_sb[:, :], sin_t[:, :]).then_inc(rope_tables_in, 16)
            sp.dma_start(wv_raw[:, :], wv[0]).then_inc(wv_in, 16)
            sp.dma_start(wq_raw[:, 1, :], wq[1]).then_inc(wq_in[1], 16)
            sp.dma_start(band_sb[:, :], band[:, :]).then_inc(tables_in, 16)
            sp.dma_start(ag_sb[:, :], a_gate[:, :]).then_inc(tables_in, 16)
            sp.dma_start(bt_sb[:, :], b_thr[:, :]).then_inc(tables_in, 16)

            def loads(g, first, last):
                for j in range(PER_GROUP):
                    if not (last and j >= 2):
                        wait(sp, wq_lo_ready, g * PER_GROUP + (j + 1))
                        sp.dma_start(wq_raw[:, j % 2, :], wq[g * PER_GROUP + (j + 2)]).then_inc(wq_in[j % 2], 16)
                    if j == 0 and not last:
                        wait(sp, wk_lo_ready, g + 1)
                        sp.dma_start(wk_raw[:, :], wk[g + 1]).then_inc(wk_in, 16)
                    if j == 1 and not last:
                        wait(sp, wv_lo_ready, g + 1)
                        sp.dma_start(wv_raw[:, :], wv[g + 1]).then_inc(wv_in, 16)
                    if j >= 2:
                        for h in (2 * j - 4, 2 * j - 3):
                            wait(sp, wo_lo_ready, g * PER_GROUP + (h - 1))
                            sp.dma_start(wo_raw[:, h % 2, :], wo[g * PER_GROUP + h]).then_inc(wo_in[h % 2], 16)

            groups(sp, loads)

            sp.wait_ge(trans_done, trans_use(LAST, 3, 1, 1) + 1)
            sp.dma_start(wb_raw, w_base[:, :]).then_inc(wb_in, 16)
            sp.wait_ge(wk_lo_ready, KV_HEADS)
            sp.dma_start(bl_sb[:, :], b_lora[:, :]).then_inc(lora_bias_in, 16)
            sp.wait_ge(wv_lo_ready, KV_HEADS)
            sp.dma_start(bb_sb[:, :], b_base[:, :]).then_inc(lora_bias_in, 16)
            for b in range(BLOCKS):
                sp.wait_ge(result_ready, b + 1)
                sp.dma_start(out[b], result[:, b % 2, :]).then_inc(out_stored[b % 2], 16)
            for s in range(2):
                sp.wait_ge(out_stored[s], 16 * (BLOCKS // 2))

        @block.tensor
        def _(pe):
            def three(bank_cols, lhs, rhs, start, stop):
                nc.tensor.matmul(bank_cols, lhs[0], rhs[0], start=start, stop=False)
                nc.tensor.matmul(bank_cols, lhs[0], rhs[1], start=False, stop=False)
                return nc.tensor.matmul(bank_cols, lhs[1], rhs[0], start=False, stop=stop)

            def project(w_hi, w_lo, t, use, w_ready, w_count, in_bank=None):
                wait(pe, w_ready, w_count)
                wait(pe, proj_taken, use - 1)
                for c in range(KT):
                    w = slice(c * D, (c + 1) * D)
                    s = slice(t * SEQ, (t + 1) * SEQ)
                    mm = three(proj_bank(t, in_bank)[:, :], (w_hi[:, w], w_lo[:, w]),
                               (xT_hi[:, c, s], xT_lo[:, c, s]), c == 0, c == KT - 1)
                mm.then_inc(proj_done, 1)

            def scores(g, j, p):
                t = p // 2
                wait(pe, q_lo_ready, g * 8 + (2 * j + t + 1))
                wait(pe, k_lo_ready, 2 * g + (t + 1))
                wait(pe, scores_masked, g * 16 + (4 * j + p - 1))
                for b in (2 * p, 2 * p + 1):
                    if b % QB == 0:
                        nc.tensor.matmul(sc_bank[p % 2][:, 0:P], rope_cos[:, t, 0:P], k_first[:, t, :],
                                         start=True, stop=True)
                        continue
                    q = slice(b * P, (b + 1) * P)
                    k = slice((b - 1) * P, (b + 1) * P)
                    mm = three(sc_bank[p % 2][:, (b % 2) * 2 * P:(b % 2 + 1) * 2 * P], (q_hi[:, q], q_lo[:, q]),
                               (k_hi[:, k], k_lo[:, k]), True, True)
                mm.then_inc(scores_done, 1)

            def transpose_probs(g, j, t):
                par = (j + 1) % 2
                wait(pe, (probs0_ready, probs1_ready)[t], g * PER_GROUP + j)
                for half in range(2):
                    use = trans_use(g, j, t, half)
                    wait(pe, trans_taken, use - 1)
                    parts = [(0, 0, 0), (1, 1, 0), (2, 1, P), (3, 2, 0)] if half == 0 else \
                            [(0, 3, P), (1, 2, P), (2, 3, 0)]
                    for slot, qb, col in parts:
                        mm = nc.tensor.transpose(tr_bank[half][:, slot * P:(slot + 1) * P],
                                                 probs[:, par, t * QB + qb, col:col + P], eye_sb[:, :])
                    mm.then_inc(trans_done, 1)

            def probs_v(g, j, t):
                use = pv_use(g, j, t)
                wait(pe, trans_taken, trans_use(g, j, t, 1) + 1)
                wait(pe, o_taken, use - 1)
                for i, (kb, slot) in enumerate(((0, 0), (2, 4), (1, 2))):
                    v = slice((t * QB + kb) * P, (t * QB + kb + 1) * P)
                    pc = slice(slot * P, (slot + 2) * P)
                    q0 = min(kb, QB - 2) * P
                    o = o_bank[t][:, q0:q0 + 2 * P]
                    for n, (a, b) in enumerate(((v_hi, pT_hi), (v_hi, pT_lo), (v_lo, pT_hi))):
                        nc.tensor.matmul(o, a[:, v], b[:, t, pc], start=(i == 0 and n == 0), stop=False,
                                         skip_group_check=True)
                mm = nc.tensor.matmul(o_bank[t][:, (QB - 1) * P:], v_last[:, t, :],
                                      pT_last[:, t, :], start=False, stop=True, skip_group_check=True)
                mm.then_inc(o_done, 1)

            def out_projection(g, b):
                use = out_use(g, b)
                wait(pe, wo_lo_ready, g * PER_GROUP)
                if b % QB == 0:
                    wait(pe, o_taken, pv_use(g, 0, b // QB) + 1)
                if not (is_group(g, E) and b < QB + 2):
                    wait(pe, o_taken, use - 1)
                for h in range(PER_GROUP):
                    mm = three(o_bank[out_bank(g, b)][:, :], (oT_hi[:, h, tok(b)], oT_lo[:, h, tok(b)]),
                               (wo_hi[:, h, :], wo_lo[:, h, :]), h == 0, h == PER_GROUP - 1)
                mm.then_inc(o_done, 1)

            def last_out_projection(b, h):
                pe.wait_ge(wo_lo_ready, LAST * PER_GROUP + h + 1)
                pe.wait_ge(o_taken, pv_use(*((LAST, h + 1) if h < 3 else (E, 0)), 0) + 1)
                if h == 0 and b < 2:
                    pe.wait_ge(proj_taken, q_proj_use(LAST, 2, 1) + 1)
                elif h == 0:
                    pe.wait_ge(scores_masked, 16 * KV_HEADS)
                mm = three(last_bank(b)[:, :], (oT_hi[:, h, tok(b)], oT_lo[:, h, tok(b)]),
                           (wo_hi[:, h, :], wo_lo[:, h, :]), h == 0, h == PER_GROUP - 1)
                if h == PER_GROUP - 1:
                    mm.then_inc(o_done, 1)

            def transpose_v(g, t):
                use = v_trans_use(g, t)
                wait(pe, proj_taken, g * PROJ_PER_GROUP + PROJ_BEFORE)
                wait(pe, trans_taken, use - 1)
                for i in range(QB):
                    mm = nc.tensor.transpose(tr_bank[t][:, i * P:(i + 1) * P], vT[:, t, i * P:(i + 1) * P],
                                             eye_sb[:, :])
                mm.then_inc(trans_done, 1)

            pe.wait_ge(constant_set, 2)
            for _ in range(12):
                nc.tensor.matmul(sc_bank[0][:, 0:P], k_first[:, 0, :], k_first[:, 0, :], start=True, stop=True)
            pe.wait_ge(eye_in, 16)

            def transpose_x(b):
                pe.wait_ge(normed_ready, b + 1)
                wait(pe, xT_lo_ready, b - 3)
                for c in range(KT):
                    mm = nc.tensor.transpose(x_bank[b % 4][:, tok(c)], normed[:, b % 4, tok(c)], eye_sb[:, :])
                mm.then_inc(xT_done, 1)

            def first_projection(use):
                t = use // 3
                if use % 3 == 0:
                    wait(pe, proj_taken, use - 1)
                    for n, (w, x_part) in enumerate(((wk_hi, xT_hi), (wk_lo, xT_hi), (wk_hi, xT_lo))):
                        if n == 0:
                            pe.wait_ge(xT_hi_ready, QB * (t + 1))
                        elif n == 1:
                            pe.wait_ge(wk_lo_ready, 1)
                        else:
                            pe.wait_ge(xT_lo_ready, QB * (t + 1))
                        for c in range(KT):
                            mm = nc.tensor.matmul(pj_bank[use % 2][:, :], w[:, tok(c)], x_part[:, c, cols(t)],
                                                  start=(n == 0 and c == 0), stop=(n == 2 and c == KT - 1))
                    mm.then_inc(proj_done, 1)
                    return
                w = (None, (wq_hi, wq_lo, wq_lo_ready), (wv_hi, wv_lo, wv_lo_ready))[use % 3]
                project(w[0], w[1], t, use, w[2], 1, use % 2)

            for b in range(QB):
                transpose_x(b)
            first_projection(0)
            first_projection(1)
            for b in range(QB, BLOCKS):
                transpose_x(b)
            for use in (2, 3, 4):
                first_projection(use)
            scores(0, 0, 0)
            scores(0, 0, 1)
            first_projection(5)

            def group_projection(g, j, t, last):
                if j == 2 and not last:
                    project(wk_hi, wk_lo, t, k_proj_use(g, t), wk_lo_ready, g + 2)
                if j == 3 and not last:
                    project(wv_hi, wv_lo, t, v_proj_use(g, t), wv_lo_ready, g + 2)

            def steps(g, first, last):
                for j in range(PER_GROUP):
                    before, after = not (first and j == 0), not (last and j == 3)
                    w_count = g * PER_GROUP + (j + 2)
                    if before:
                        scores(g, j, 0)
                        scores(g, j, 1)
                        transpose_probs(g, j, 0)
                    if after:
                        project(wq_hi, wq_lo, 0, q_proj_use(g, j, 0), wq_lo_ready, w_count)
                    if last and j == 3:
                        for h in (0, 1):
                            for b in (0, 1):
                                last_out_projection(b, h)
                    scores(g, j, 2)
                    scores(g, j, 3)
                    if first and j == 0:
                        transpose_v(g, 0)
                        transpose_v(g, 1)
                    if before:
                        transpose_probs(g, j, 1)
                    if j == 1:
                        wait(pe, trans_taken, v_trans_use(g, 1) + 1)
                    if before:
                        probs_v(g, j, 0)
                    if j == 1 and not first:
                        out_projection(g, 4)
                    if after:
                        project(wq_hi, wq_lo, 1, q_proj_use(g, j, 1), wq_lo_ready, w_count)
                    if j == 1 and not first:
                        for b in (5, 6, 7):
                            out_projection(g, b)
                    group_projection(g, j, 0, last)
                    if last and j == 3:
                        for h in (0, 1):
                            for b in (2, 3):
                                last_out_projection(b, h)
                    if before:
                        probs_v(g, j, 1)
                    group_projection(g, j, 1, last)
                    if j == 0 and not first:
                        transpose_v(g, 0)
                        transpose_v(g, 1)
                        for b in range(QB):
                            out_projection(g, b)

            groups(pe, steps)
            for t in range(BATCH):
                transpose_probs(E, 0, t)
                if t == 0:
                    for b in (0, 1):
                        last_out_projection(b, 2)
            for t in range(BATCH):
                probs_v(E, 0, t)
                if t == 0:
                    for b in (2, 3):
                        last_out_projection(b, 2)

            def transpose_y(b):
                pe.wait_ge(y_normed, b + 1)
                if b >= 2:
                    pe.wait_ge(yT_ready, b - 1)
                else:
                    pe.wait_ge(trans_taken, trans_use(E, 0, 1, 1) + 1)
                for c in range(KT):
                    mm = nc.tensor.transpose(tr_bank[b % 2][:, tok(c)], normed[:, b % 4, tok(c)], eye_sb[:, :])
                mm.then_inc(yT_done, 1)

            def down_and_gate(b):
                pe.wait_ge(yT_ready, b + 1)
                if b % QB == 0:
                    pe.wait_ge(o_taken, out_use(E, 3) + 1)
                    wait(pe, lora_scaled, b // QB)
                i = b % QB
                for c in range(KT):
                    mm = nc.tensor.matmul(sc_bank[i // 2][:, (i % 2) * GCOLS:(i % 2 + 1) * GCOLS],
                                          yT(b)[:, tok(c)], ag_sb[:, c * GCOLS:(c + 1) * GCOLS],
                                          start=c == 0, stop=c == KT - 1)
                mm.then_inc(down_done, 1)

            def transpose_lora(t):
                pe.wait_ge(lora_scaled, t + 1)
                if t == 0:
                    pe.wait_ge(o_taken, out_use(E, 6) + 1)
                else:
                    pe.wait_ge(loraT_ready, t)
                for i in range(QB):
                    mm = nc.tensor.transpose(o_bank[0][:, tok(i)], lora_h[:, i, :], eye_sb[:, :])
                mm.then_inc(loraT_done, 1)

            def base(b):
                pe.wait_ge(wb_lo_ready, KT)
                pe.wait_ge(yT_lo_ready, b + 1)
                if b < 6:
                    wait(pe, result_ready, b - 1)
                for c in range(KT):
                    w = slice(c % 2 * HIDDEN, (c % 2 + 1) * HIDDEN)
                    three(ffn_bank(b)[:, :], (xT_hi[:, c, tok(b)], xT_lo[:, c, tok(b)]),
                          (wb_hi[c // 2][:, w], wb_lo[c // 2][:, w]), c == 0, False)

            def lora(b):
                pe.wait_ge(loraT_ready, b // QB + 1)
                nc.tensor.matmul(ffn_bank(b)[:, :], lora_hT[:, b % QB, :], bl_sb[:, :], start=False,
                                 stop=True).then_inc(ffn_done, 1)

            for b in range(QB):
                last_out_projection(b, 3)
            out_projection(E, QB)
            for i in range(QB):
                if i < QB - 1:
                    out_projection(E, QB + i + 1)
                transpose_y(i)
                if i >= 2:
                    down_and_gate(i - 2)
            down_and_gate(2)
            down_and_gate(3)
            pe.wait_ge(o_taken, out_use(E, 1) + 1)
            pe.wait_ge(lora_bias_in, 16 * 2)
            base(0)
            transpose_y(4)
            base(1)
            transpose_y(5)
            transpose_lora(0)
            down_and_gate(4)
            lora(0)
            lora(1)
            transpose_y(6)
            base(2)
            lora(2)
            transpose_y(7)
            base(3)
            lora(3)
            for b in range(QB + 1, BLOCKS):
                down_and_gate(b)
            base(4)
            base(5)
            transpose_lora(1)
            base(6)
            for b in (4, 5, 6):
                lora(b)
            base(7)
            lora(7)

        @block.scalar
        def _(act):
            def copy(dst, src):
                return nc.scalar.activation(dst, src, ACT.Copy)

            def exp_pair(g, j, p):
                act.wait_ge(shift_ready, g * 16 + (4 * j + p + 1))
                for b in (2 * p, 2 * p + 1):
                    s = probs[:, j % 2, b, 0:P if b % QB == 0 else 2 * P]
                    last = nc.scalar.activation(s, s, ACT.Exp, bias=shift[:, j % 2, b:b + 1], scale=SM_SCALE,
                                                accum_out=row_sum[:, j % 2, b:b + 1])
                last.then_inc(exp_done, 1)

            def pT_split(g, j, t):
                wait(act, o_done, pv_use(g, j - 1, t) + 1 if j else pv_use(g - 1, 3, t) + 1)
                act.wait_ge(trans_done, trans_use(g, j, t, 0) + 1)
                copy(pT_hi[:, t, 0:4 * P], tr_bank[0][:, :]).then_inc(pT_hi_ready, 1)
                act.wait_ge(trans_done, trans_use(g, j, t, 1) + 1)
                copy(pT_hi[:, t, 4 * P:6 * P], tr_bank[1][:, P:3 * P]).then_inc(pT_hi_ready, 1)

            def swap(t, use, rope_use, in_bank=None):
                src = proj_bank(t, in_bank)
                act.wait_ge(proj_done, use + 1)
                wait(act, rope_added, rope_use - 1)
                copy(rope_sin[0:half, t, :], src[half:D, :])
                copy(rope_sin[half:D, t, :], src[0:half, :]).then_inc(rope_swapped, 1)

            def k_swap(t, use, rope_use, in_bank=None):
                src = proj_bank(t, in_bank)
                act.wait_ge(proj_done, use + 1)
                wait(act, k_added, rope_use - 1)
                copy(k_sin[0:half, t, :], src[half:D, :])
                copy(k_sin[half:D, t, :], src[0:half, :]).then_inc(k_swapped, 1)

            def k_split(t, count):
                act.wait_ge(k_added, count)
                copy(k_hi[:, cols(t)], k_rot[:, t, :]).then_inc(k_hi_ready, 1)

            def q_split(g, j, t):
                act.wait_ge(rope_added, q_rope_use(g, j, t) + 1)
                act.wait_ge(scores_done, g * 16 + (4 * j + 2 * t + 2))
                copy(q_hi[:, cols(t)], rope_cos[:, t, :]).then_inc(q_hi_ready, 1)

            def wo_split(g, j):
                for h in (2 * j - 4, 2 * j - 3):
                    act.wait_ge(wo_in[h % 2], (g * 2 + (h // 2 + 1)) * 16)
                    wait(act, o_done, out_use(g, 7) + 1)
                    copy(wo_hi[:, h, :], wo_raw[:, h % 2, :]).then_inc(wo_hi_ready, 1)

            def v_split(g):
                for t in range(BATCH):
                    act.wait_ge(trans_done, v_trans_use(g, t) + 1)
                    copy(v_last[:, t, :], tr_bank[t][:, 3 * P:])
                    copy(v_hi[:, split_keys(t)], tr_bank[t][:, 0:3 * P]).then_inc(v_hi_ready, 1)

            def o_split(g, j, t):
                act.wait_ge(o_done, pv_use(g, j, t) + 1)
                copy(oT_hi[:, (j - 1) % PER_GROUP, cols(t)], o_bank[t][:, :]).then_inc(oT_hi_ready, 1)

            def x_split(b):
                act.wait_ge(xT_done, b + 1)
                copy(xT_hi[:, :, tok(b)], x_bank[b % 4][:, :].rearrange("p (c n) -> p c n", c=KT))\
                    .then_inc(xT_hi_ready, 1)

            def first_q_split(t):
                act.wait_ge(rope_added, t + 1)
                copy(q_hi[:, cols(t)], rope_cos[:, t, :]).then_inc(q_hi_ready, 1)

            x_split(0)
            x_split(1)
            act.wait_ge(wk_in, 16)
            copy(wk_hi[:, :], wk_raw[:, :]).then_inc(wk_hi_ready, 1)
            x_split(2)
            act.wait_ge(wq_in[0], 16)
            copy(wq_hi[:, :], wq_raw[:, 0, :]).then_inc(wq_hi_ready, 1)
            x_split(3)
            act.wait_ge(wv_in, 16)
            copy(wv_hi[:, :], wv_raw[:, :]).then_inc(wv_hi_ready, 1)
            k_swap(0, 0, 0, 0)
            x_split(4)
            x_split(5)
            swap(0, 1, 0, 1)
            x_split(6)
            x_split(7)
            k_split(0, 1)
            first_q_split(0)
            k_swap(1, 3, 1, 1)
            swap(1, 4, 1, 0)
            act.wait_ge(wq_in[1], 16)
            copy(wq_hi[:, :], wq_raw[:, 1, :]).then_inc(wq_hi_ready, 1)
            k_split(1, 2)
            exp_pair(0, 0, 0)
            exp_pair(0, 0, 1)
            first_q_split(1)

            def steps(g, first, last):
                for j in range(PER_GROUP):
                    before, after = not (first and j == 0), not (last and j == 3)
                    if before:
                        exp_pair(g, j, 0)
                        pT_split(g, j, 0)
                        exp_pair(g, j, 1)
                    if j >= 2 and last:
                        wo_split(g, j)
                    if after:
                        swap(0, q_proj_use(g, j, 0), q_rope_use(g, j, 0))
                    exp_pair(g, j, 2)
                    if before:
                        pT_split(g, j, 1)
                    exp_pair(g, j, 3)
                    if j == 3 and not last:
                        for t in range(BATCH):
                            act.wait_ge(scores_done, g * 16 + (12 + 2 * t + 2))
                            k_split(t, k_rope_use(g + 1, t) + 1)
                    if before:
                        o_split(g, j, 0)
                    if after:
                        q_split(g, j, 0)
                        if first and j == 0:
                            v_split(g)
                        swap(1, q_proj_use(g, j, 1), q_rope_use(g, j, 1))
                    if not (last and j >= 2):
                        act.wait_ge(wq_in[j % 2], (g * 2 + (j // 2 + 2)) * 16)
                        act.wait_ge(proj_done, q_proj_use(g, j, 1) + 1)
                        copy(wq_hi[:, :], wq_raw[:, j % 2, :]).then_inc(wq_hi_ready, 1)
                    if before:
                        o_split(g, j, 1)
                    if after:
                        q_split(g, j, 1)
                    if j == 2 and not last:
                        k_swap(0, k_proj_use(g, 0), k_rope_use(g + 1, 0))
                    if j == 0 and not first:
                        v_split(g)
                    if j == 0 and not last:
                        act.wait_ge(wk_in, (g + 2) * 16)
                        copy(wk_hi[:, :], wk_raw[:, :]).then_inc(wk_hi_ready, 1)
                    if j == 1 and not last:
                        act.wait_ge(wv_in, (g + 2) * 16)
                        copy(wv_hi[:, :], wv_raw[:, :]).then_inc(wv_hi_ready, 1)
                    if j >= 2 and not last:
                        wo_split(g, j)
                    if j == 2 and not last:
                        k_swap(1, k_proj_use(g, 1), k_rope_use(g + 1, 1))

            groups(act, steps)
            for t in range(BATCH):
                pT_split(E, 0, t)
            for t in range(BATCH):
                o_split(E, 0, t)
            act.wait_ge(wb_in, 16)
            for n in range(2):
                copy(wb_hi[n][:, :], wb_raw[:, n * TOKENS:(n + 1) * TOKENS]).then_inc(wb_hi_ready, 1)

            def y_split(b):
                act.wait_ge(yT_done, b + 1)
                wait(act, down_done, b - 3)
                wait(act, yT_lo_ready, b - 3)
                copy(yT(b), tr_bank[b % 2][:, :]).then_inc(yT_ready, 1)
                act.wait_ge(yT_ready, b + 1)
                copy(xT_hi[:, :, tok(b)], yT(b).rearrange("p (c n) -> p c n", c=KT)).then_inc(yT_hi_ready, 1)

            def gate_exp(t):
                act.wait_ge(logits_ready, t + 1)
                nc.scalar.activation(gexp[:, :, :], logit[:, :, :], ACT.Exp).then_inc(gexp_done, 1)

            def lora_copy(t):
                act.wait_ge(loraT_done, t + 1)
                wait(act, ffn_done, QB * t)
                copy(lora_hT, o_bank[0][:, :].rearrange("p (a b) -> p a b", a=QB)).then_inc(loraT_ready, 1)

            for b in range(QB):
                y_split(b)
            gate_exp(0)
            y_split(4)
            y_split(5)
            lora_copy(0)
            y_split(6)
            y_split(7)
            gate_exp(1)
            lora_copy(1)

        @block.gpsimd
        def _(pool):
            nc.gpsimd.memset(k_first[:, 0, :], 0.0).then_inc(constant_set, 1)
            nc.gpsimd.memset(minus_half[:, :], -0.5).then_inc(constant_set, 1)
            pool.wait_ge(constant_set, 2)

            def low(raw, hi, lo, hi_ready, count, lo_ready):
                pool.wait_ge(hi_ready, count)
                nc.gpsimd.tensor_tensor(lo, raw, hi.bitcast(F32), ALU.subtract).then_inc(lo_ready, 1)

            def wq_low(slot, count):
                low(wq_raw[:, slot, :], wq_hi[:, :], wq_lo[:, :], wq_hi_ready, count, wq_lo_ready)

            def block_rstd(b, count):
                pool.wait_ge(moments_ready, count)
                nc.gpsimd.tensor_scalar(var_eps[:, b:b + 1], moments[:, b, 1:2], EPS, None, ALU.add)\
                    .then_inc(var_ready, 1)
                pool.wait_ge(var_ready, count)
                nc.gpsimd.tensor_tensor(rstd[:, b:b + 1], var_eps[:, b:b + 1], minus_half[:, :], ALU.pow)\
                    .then_inc(rstd_ready, 1)

            def k_low(t, count):
                pool.wait_ge(k_hi_ready, count)
                nc.gpsimd.tensor_tensor(k_lo[:, cols(t)], k_rot[:, t, :], f32(k_hi[:, cols(t)]), ALU.subtract)
                nc.gpsimd.tensor_copy(k_first[:, t, :], k_rot[:, t, 0:P]).then_inc(k_lo_ready, 1)

            def k_rope(t, cos_use, rope_use):
                pool.wait_ge(k_swapped, rope_use + 1)
                nc.gpsimd.tensor_tensor(k_sin[:, t, :], k_sin[:, t, :], sin_sb[:, :], ALU.mult).then_inc(k_scaled, 1)
                pool.wait_ge(k_scaled, rope_use + 1)
                pool.wait_ge(proj_taken, cos_use + 1)
                nc.gpsimd.tensor_tensor(k_rot[:, t, :], k_rot[:, t, :], k_sin[:, t, :], ALU.add).then_inc(k_added, 1)

            for b in range(QB):
                block_rstd(b, b + 1)
            low(wk_raw[:, :], wk_hi[:, :], wk_lo[:, :], wk_hi_ready, 1, wk_lo_ready)
            wq_low(0, 1)
            for b in range(QB, BLOCKS):
                block_rstd(b, b + 1)
            low(wv_raw[:, :], wv_hi[:, :], wv_lo[:, :], wv_hi_ready, 1, wv_lo_ready)
            pool.wait_ge(rope_tables_in, 16 * 2)
            k_rope(0, 0, 0)
            k_low(0, 1)
            k_rope(1, 3, 1)
            wq_low(1, 2)
            k_low(1, 2)

            def wo_low(g, j):
                for h in (2 * j - 4, 2 * j - 3):
                    low(wo_raw[:, h % 2, :], wo_hi[:, h, :], wo_lo[:, h, :], wo_hi_ready,
                        g * PER_GROUP + (h + 1), wo_lo_ready)

            def normalise(g, j, t):
                pool.wait_ge(inv_ready, g * 8 + (2 * j + t + 1))
                b = t * QB
                s = probs[:, j % 2, b, 0:P]
                nc.gpsimd.tensor_tensor(s, s, inv_sum[:, j % 2, b:b + 1].to_broadcast([P, P]), ALU.mult)
                s = probs[:, j % 2, b + 1:b + QB, :]
                inv = inv_sum[:, j % 2, b + 1:b + QB].unsqueeze(2).to_broadcast([P, QB - 1, 2 * P])
                nc.gpsimd.tensor_tensor(s, s, inv, ALU.mult).then_inc(probs1_ready, 1)

            def steps(g, first, last):
                for j in range(PER_GROUP):
                    if j == 3 and not last:
                        for t in range(BATCH):
                            k_rope(t, k_proj_use(g, t), k_rope_use(g + 1, t))
                        for t in range(BATCH):
                            k_low(t, 2 * g + (t + 3))
                    if not (last and j >= 2):
                        wq_low(j % 2, g * PER_GROUP + (j + 3))
                    if last and j >= 2:
                        wo_low(g, j)
                    if not (last and j == 3):
                        normalise(g, j, 1)
                    if j == 0 and not last:
                        low(wk_raw[:, :], wk_hi[:, :], wk_lo[:, :], wk_hi_ready, g + 2, wk_lo_ready)
                    if j == 1 and not last:
                        low(wv_raw[:, :], wv_hi[:, :], wv_lo[:, :], wv_hi_ready, g + 2, wv_lo_ready)
                    if j >= 2 and not last:
                        wo_low(g, j)

            groups(pool, steps)
            for b in range(BLOCKS):
                block_rstd(b, BLOCKS + b + 1)
                if b < KT:
                    w = slice(b * HIDDEN, (b + 1) * HIDDEN)
                    part = slice(b % 2 * HIDDEN, (b % 2 + 1) * HIDDEN)
                    low(wb_raw[:, w], wb_hi[b // 2][:, part], wb_lo[b // 2][:, part], wb_hi_ready, b // 2 + 1,
                        wb_lo_ready)
            pool.wait_ge(lora_bias_in, 16 * 2)
            for b in range(BLOCKS):
                pool.wait_ge(y_normed, b + 1)
                nc.gpsimd.tensor_tensor(resid[:, b, :], resid[:, b, :], bb_sb[:, :], ALU.add)\
                    .then_inc(bias_added, 1)

        @block.vector
        def _(dve):
            TT = nc.vector.tensor_tensor

            def mask_pair(g, j, p):
                dve.wait_ge(scores_done, g * 16 + (4 * j + p + 1))
                nc.vector.memset(gap[:, :], 0.0)
                for b in (2 * p, 2 * p + 1):
                    w = P if b % QB == 0 else 2 * P
                    c0 = (b % 2) * 2 * P
                    last = nc.vector.tensor_tensor_reduce(
                        out=probs[:, j % 2, b, 0:w], in0=sc_bank[p % 2][:, c0:c0 + w],
                        in1=band_sb[:, 2 * P - w:2 * P], scale=1.0, scalar=LOWEST, op0=ALU.add, op1=ALU.max,
                        accum_out=row_max[:, j % 2, b:b + 1])
                last.then_inc(scores_masked, 1)

            def shift_pair(g, j, p):
                n = g * 16 + (4 * j + p + 1)
                dve.wait_ge(scores_masked, n)
                nc.vector.tensor_scalar(shift[:, j % 2, 2 * p:2 * p + 2], row_max[:, j % 2, 2 * p:2 * p + 2],
                                        -SM_SCALE, None, ALU.mult).then_inc(shift_ready, 1)

            def normalise(g, j, t):
                n = g * 8 + (2 * j + t + 1)
                dve.wait_ge(exp_done, g * 16 + (4 * j + 2 * t + 2))
                bs = slice(t * QB, (t + 1) * QB)
                nc.vector.reciprocal(inv_sum[:, j % 2, bs], row_sum[:, j % 2, bs]).then_inc(inv_ready, 1)
                if t and not (j == 3 and is_group(g, LAST)):
                    return
                dve.wait_ge(inv_ready, n)
                for b in range(t * QB, (t + 1) * QB):
                    s = probs[:, j % 2, b, 0:P if b % QB == 0 else 2 * P]
                    last = nc.vector.tensor_scalar(s, s, inv_sum[:, j % 2, b:b + 1], None, ALU.mult)
                last.then_inc((probs0_ready, probs1_ready)[t], 1)

            def pT_low(g, j, t):
                n = g * 16 + (4 * j - 4 + 2 * t + 1)
                dve.wait_ge(pT_hi_ready, n)
                c = slice(0, 4 * P)
                TT(pT_lo[:, t, c], tr_bank[0][:, :], f32(pT_hi[:, t, c]), ALU.subtract).then_inc(trans_taken, 1)
                dve.wait_ge(pT_hi_ready, n + 1)
                nc.vector.tensor_copy(pT_last[:, t, :], tr_bank[1][:, 0:P])
                c = slice(4 * P, 6 * P)
                TT(pT_lo[:, t, c], tr_bank[1][:, P:3 * P], f32(pT_hi[:, t, c]), ALU.subtract)\
                    .then_inc(trans_taken, 1)

            def rope(dst, t, use, rope_use, in_bank=None):
                dve.wait_ge(rope_swapped, rope_use + 1)
                TT(dst[:, t, :], proj_bank(t, in_bank)[:, :], cos_sb[:, :], ALU.mult)\
                    .then_inc(proj_taken, 1)
                TT(rope_sin[:, t, :], rope_sin[:, t, :], sin_sb[:, :], ALU.mult).then_inc(rope_scaled, 1)

            def k_cos(t, rope_use, in_bank=None):
                dve.wait_ge(k_swapped, rope_use + 1)
                TT(k_rot[:, t, :], proj_bank(t, in_bank)[:, :], cos_sb[:, :], ALU.mult)\
                    .then_inc(proj_taken, 1)

            def rope_add(dst, t, use, rope_use):
                dve.wait_ge(proj_taken, use + 1)
                dve.wait_ge(rope_scaled, rope_use + 1)
                TT(dst[:, t, :], dst[:, t, :], rope_sin[:, t, :], ALU.add).then_inc(rope_added, 1)

            def q_low(count, t):
                dve.wait_ge(q_hi_ready, count)
                TT(q_lo[:, cols(t)], rope_cos[:, t, :], f32(q_hi[:, cols(t)]), ALU.subtract).then_inc(q_lo_ready, 1)

            def o_low(g, j, t):
                dve.wait_ge(oT_hi_ready, g * 8 + (2 * j - 2 + t + 1))
                h = (j - 1) % PER_GROUP
                TT(oT_lo[:, h, cols(t)], o_bank[t][:, :], f32(oT_hi[:, h, cols(t)]), ALU.subtract)\
                    .then_inc(o_taken, 1)

            def v_low(g):
                for t in range(BATCH):
                    dve.wait_ge(v_hi_ready, 2 * g + (t + 1))
                    keys = split_keys(t)
                    TT(v_lo[:, keys], tr_bank[t][:, 0:3 * P], f32(v_hi[:, keys]), ALU.subtract)\
                        .then_inc(trans_taken, 1)

            def add_out(g, b):
                dve.wait_ge(o_done, out_use(g, b) + 1)
                src = last_bank(b) if is_group(g, E) else o_bank[out_bank(g, b)]
                TT(resid[:, b, :], src[:, :], resid[:, b, :], ALU.add).then_inc(o_taken, 1)

            def v_copy(t, use, in_bank=None):
                dve.wait_ge(proj_done, use + 1)
                nc.vector.tensor_copy(vT[:, t, :], proj_bank(t, in_bank)[:, :])\
                    .then_inc(proj_taken, 1)

            lns = [0]

            def chain(ins):
                lns[0] += 1
                ins.then_inc(ln_step, 1)
                dve.wait_ge(ln_step, lns[0])

            def block_moments(b):
                chain(nc.vector.bn_stats(stats[:, b, :], resid[:, b, :]))
                nc.vector.bn_aggr(moments[:, b, :], stats[:, b, :]).then_inc(moments_ready, 1)

            def normalise_block(b, count, free, ready):
                dve.wait_ge(rstd_ready, count)
                wait(dve, free, b - 3)
                nc.vector.tensor_scalar(normed[:, b % 4, :], resid[:, b, :], moments[:, b, 0:1], rstd[:, b:b + 1],
                                        ALU.subtract, ALU.mult).then_inc(ready, 1)

            def split_x(b):
                dve.wait_ge(xT_hi_ready, b + 1)
                TT(xT_lo[:, :, tok(b)], x_bank[b % 4][:, :].rearrange("p (c n) -> p c n", c=KT),
                   f32(xT_hi[:, :, tok(b)]), ALU.subtract).then_inc(xT_lo_ready, 1)

            def yT_low(b):
                dve.wait_ge(yT_hi_ready, b + 1)
                TT(xT_lo[:, :, tok(b)], yT(b).rearrange("p (c n) -> p c n", c=KT), f32(xT_hi[:, :, tok(b)]),
                   ALU.subtract).then_inc(yT_lo_ready, 1)

            def load_moments(b):
                dve.wait_ge(x_in[b], 16)
                block_moments(b)

            def normalise_x(b):
                normalise_block(b, b + 1, xT_done, normed_ready)

            load_moments(0)
            load_moments(1)
            normalise_x(0)
            load_moments(2)
            normalise_x(1)
            load_moments(3)
            normalise_x(2)
            split_x(0)
            normalise_x(3)
            split_x(1)
            split_x(2)
            split_x(3)
            for b in range(QB, BLOCKS):
                load_moments(b)
            normalise_x(4)
            normalise_x(5)
            dve.wait_ge(rope_tables_in, 16 * 2)
            k_cos(0, 0, 0)
            normalise_x(6)
            normalise_x(7)
            split_x(4)
            split_x(5)
            rope(rope_cos, 0, 1, 0, 1)
            split_x(6)
            split_x(7)
            v_copy(0, 2, 0)
            rope_add(rope_cos, 0, 1, 0)
            q_low(1, 0)
            k_cos(1, 1, 1)
            dve.wait_ge(tables_in, 16 * TABLES)
            mask_pair(0, 0, 0)
            shift_pair(0, 0, 0)
            rope(rope_cos, 1, 4, 1, 0)
            mask_pair(0, 0, 1)
            shift_pair(0, 0, 1)
            rope_add(rope_cos, 1, 4, 1)
            q_low(2, 1)
            v_copy(1, 5, 1)

            def steps(g, first, last):
                for j in range(PER_GROUP):
                    before, after = not (first and j == 0), not (last and j == 3)
                    use = [q_proj_use(g, j, t) for t in range(BATCH)]
                    rot = [q_rope_use(g, j, t) for t in range(BATCH)]
                    if before:
                        mask_pair(g, j, 0)
                        shift_pair(g, j, 0)
                        mask_pair(g, j, 1)
                        shift_pair(g, j, 1)
                    if j == 3 and not last:
                        k_cos(1, k_rope_use(g + 1, 1))
                    if before:
                        pT_low(g, j, 0)
                    if not (first and j == 0):
                        normalise(g, j, 0)
                    mask_pair(g, j, 2)
                    shift_pair(g, j, 2)
                    if first and j == 0:
                        rope(rope_cos, 0, use[0], rot[0])
                    mask_pair(g, j, 3)
                    shift_pair(g, j, 3)
                    if first and j == 0:
                        rope_add(rope_cos, 0, use[0], rot[0])
                        normalise(g, j, 0)
                    elif after:
                        rope(rope_cos, 0, use[0], rot[0])
                    if before:
                        pT_low(g, j, 1)
                    if after and before:
                        rope_add(rope_cos, 0, use[0], rot[0])
                    if before:
                        o_low(g, j, 0)
                    if j == 1 and not first:
                        add_out(g, 4)
                    if after:
                        q_low(g * 8 + (2 * j + 3), 0)
                        if first and j == 0:
                            v_low(g)
                        rope(rope_cos, 1, use[1], rot[1])
                        rope_add(rope_cos, 1, use[1], rot[1])
                    if j == 1 and not first:
                        for b in (5, 6, 7):
                            add_out(g, b)
                    if before:
                        o_low(g, j, 1)
                    normalise(g, j, 1)
                    if after:
                        q_low(g * 8 + (2 * j + 4), 1)
                    if j == 0 and not first:
                        v_low(g)
                        for b in range(QB):
                            add_out(g, b)
                    if j == 2 and not last:
                        k_cos(0, k_rope_use(g + 1, 0))
                    if j == 3 and not last:
                        for t in range(BATCH):
                            v_copy(t, v_proj_use(g, t))

            groups(dve, steps)
            for t in range(BATCH):
                pT_low(E, 0, t)
            for t in range(BATCH):
                o_low(E, 0, t)

            def gates(t):
                dve.wait_ge(down_done, QB * (t + 1))
                for k in range(2):
                    v = sc_bank[k][:, 0:2 * GCOLS].rearrange("p (a b) -> p a b", a=2)
                    last = nc.vector.tensor_copy(logit[:, 2 * k:2 * k + 2, :], v[:, :, ER:GCOLS])
                chain(last)
                z = logit[:, :, EXPERTS]
                chain(nc.vector.tensor_reduce(gmax[:, :], logit[:, :, 0:EXPERTS], AX.X, ALU.max))
                nc.vector.tensor_scalar(z, z, bt_sb[:, 0:1], -1.0, ALU.add, ALU.mult)
                TT(logit[:, :, 0:EXPERTS], logit[:, :, 0:EXPERTS], gmax[:, :].unsqueeze(2).to_broadcast([P, QB, EXPERTS]),
                   ALU.subtract).then_inc(logits_ready, 1)
                dve.wait_ge(gexp_done, t + 1)
                e = gexp[:, :, 0:EXPERTS]
                chain(nc.vector.tensor_reduce(gsum[:, :], e, AX.X, ALU.add))
                chain(nc.vector.reciprocal(ginv[:, :], gsum[:, :]))
                chain(nc.vector.tensor_scalar(thr[:, :], gexp[:, :, EXPERTS], 1.0, None, ALU.add))
                chain(nc.vector.reciprocal(thr[:, :], thr[:, :]))
                chain(nc.vector.tensor_scalar(thr[:, :], thr[:, :], MAX_THRESHOLD, None, ALU.mult))

                def wide(a):
                    return a[:, :].unsqueeze(2).to_broadcast([P, QB, EXPERTS])

                chain(TT(gate[:, :, :], e, wide(ginv), ALU.mult))
                chain(TT(gate[:, :, :], gate[:, :, :], wide(thr), ALU.subtract))
                chain(nc.vector.tensor_scalar(gate[:, :, :], gate[:, :, :], 0.0, None, ALU.max))
                chain(nc.vector.tensor_reduce(gsum[:, :], gate[:, :, :], AX.X, ALU.add))
                chain(nc.vector.tensor_scalar(iszero[:, :], gsum[:, :], 0.0, None, ALU.is_equal))
                chain(TT(gsum[:, :], gsum[:, :], iszero[:, :], ALU.add))
                chain(nc.vector.reciprocal(ginv[:, :], gsum[:, :]))
                chain(nc.vector.tensor_scalar(ginv[:, :], ginv[:, :], LORA_SCALING, None, ALU.mult))
                chain(TT(gate[:, :, :], gate[:, :, :], wide(ginv), ALU.mult))
                wait(dve, loraT_done, t)
                for i in range(QB):
                    c0 = (i % 2) * GCOLS
                    last = TT(lora_h[:, i, :].rearrange("p (e r) -> p e r", e=EXPERTS),
                              sc_bank[i // 2][:, c0:c0 + ER].rearrange("p (e r) -> p e r", e=EXPERTS),
                              gate[:, i, :].unsqueeze(2).to_broadcast([P, EXPERTS, RANK]), ALU.mult)
                last.then_inc(lora_scaled, 1)

            def finish(b):
                dve.wait_ge(ffn_done, b + 1)
                dve.wait_ge(bias_added, b + 1)
                if b >= 2:
                    dve.wait_ge(out_stored[b % 2], 16 * (b // 2))
                TT(result[:, b % 2, :], ffn_bank(b)[:, :], resid[:, b, :], ALU.add).then_inc(result_ready, 1)

            for b in range(BLOCKS):
                if 3 <= b < 7:
                    normalise_block(b - 3, BLOCKS + b - 2, yT_done, y_normed)
                add_out(E, b)
                if b >= 4:
                    yT_low(b - 4)
                dve.wait_ge(o_taken, out_use(E, b) + 1)
                block_moments(b)
            for b in (4, 5):
                normalise_block(b, BLOCKS + b + 1, yT_done, y_normed)
            gates(0)
            yT_low(4)
            normalise_block(6, BLOCKS + 7, yT_done, y_normed)
            yT_low(5)
            normalise_block(7, BLOCKS + 8, yT_done, y_normed)
            finish(0)
            finish(1)
            yT_low(6)
            finish(2)
            yT_low(7)
            finish(3)
            gates(1)
            for b in range(QB, BLOCKS):
                finish(b)


def kernel(L0_attn_x, L0_attn_wq, L0_attn_wk, L0_attn_wv, L0_attn_wo, L0_ffn_W_base, L0_ffn_b_base, L0_ffn_W_gate,
           L0_ffn_W_thr, L0_ffn_b_thr, L0_ffn_A_w, L0_ffn_B_w):
    import concourse.bacc as bacc
    from concourse.bass_utils import run_bass_kernel_spmd

    def lay(a):
        return np.ascontiguousarray(a)

    def heads_first(w, heads):
        return lay(np.asarray(w).reshape(KT, P, heads, D).transpose(2, 1, 0, 3).reshape(heads, P, KT * D))

    def channel_tiles(w):
        w = np.asarray(w)
        return lay(w.reshape(KT, P, w.shape[1]).transpose(1, 0, 2).reshape(P, KT * w.shape[1]))

    inv_freq = np.float32(10000.0) ** (-np.arange(D // 2, dtype=np.float32) / np.float32(D // 2))
    angle = inv_freq.astype(np.float32)[:, None] * np.arange(SEQ, dtype=np.float32)[None, :]
    cos_t = np.concatenate([np.cos(angle), np.cos(angle)]).astype(np.float32)
    sin_t = np.concatenate([-np.sin(angle), np.sin(angle)]).astype(np.float32)
    i, jj = np.arange(P)[:, None], np.arange(P)[None, :]
    band = np.concatenate([np.where(jj > i, 0.0, MASKED), np.where(jj <= i, 0.0, MASKED)], axis=1).astype(np.float32)

    a_w = np.asarray(L0_ffn_A_w).reshape(ER, HIDDEN)
    a_gate = np.concatenate([a_w, np.asarray(L0_ffn_W_gate), np.asarray(L0_ffn_W_thr)[None, :]]).T
    ins = {
        "x": lay(np.asarray(L0_attn_x).reshape(BLOCKS, P, HIDDEN)),
        "wq": heads_first(L0_attn_wq, HEADS),
        "wk": heads_first(L0_attn_wk, KV_HEADS),
        "wv": heads_first(L0_attn_wv, KV_HEADS),
        "wo": lay(np.asarray(L0_attn_wo).reshape(HEADS, D, HIDDEN)),
        "w_base": channel_tiles(np.asarray(L0_ffn_W_base).T),
        "b_base": lay(np.broadcast_to(np.asarray(L0_ffn_b_base)[None, :], (P, HIDDEN))),
        "a_gate": channel_tiles(a_gate),
        "b_thr": lay(np.broadcast_to(np.asarray(L0_ffn_b_thr)[None, :], (P, 1))),
        "b_lora": lay(np.asarray(L0_ffn_B_w).transpose(0, 2, 1).reshape(ER, HIDDEN)),
        "cos_t": cos_t,
        "sin_t": sin_t,
        "band": band,
        "eye": np.eye(P, dtype=np.float32),
    }
    nc = bacc.Bacc("TRN2", target_bir_lowering=False, num_devices=1)
    arrays, args = {}, []
    for name, a in ins.items():
        arrays[f"in_{name}"] = a
        args.append(nc.dram_tensor(f"in_{name}", a.shape, F32, kind="ExternalInput").ap())
    res = nc.dram_tensor("layer_out", (BLOCKS, P, HIDDEN), F32, kind="ExternalOutput").ap()
    layer_kernel(nc, *args, res)
    r = run_bass_kernel_spmd(nc, [arrays], core_ids=[0])
    return r.results[0]["layer_out"].reshape(BATCH, SEQ, HIDDEN)
```
